# Optimizing a Trainium2 kernel written in Bass

```python
import numpy as np
import jax
import jax.numpy as jnp

def _softmax(x, axis=-1):
    return jax.nn.softmax(x, axis=axis)

def _gelu(x):
    return jax.nn.gelu(x, approximate=True)

def _silu(x):
    return jax.nn.silu(x)

def _sigmoid(x):
    return jax.nn.sigmoid(x)

def _layernorm(x, axis=-1, eps=1e-05):
    m = jnp.mean(x, axis=axis, keepdims=True)
    v = jnp.var(x, axis=axis, keepdims=True)
    return (x - m) / jnp.sqrt(v + eps)

def _scatter_add(tgt, idx, src, axis=0):
    return tgt.at[idx].add(src)

def _segment_sum(src, seg, n):
    return jax.ops.segment_sum(src, seg, n)
kernel_name = 'mk_adaln_attn_ffn_d1_seqx_r8_bdf6f3'

def setup_inputs(seed: int=0):
    np.random.seed(seed)
    _w = jnp.asarray

    def _rec_inputs():
        import jax
        import jax.numpy as jnp
        _rk = jax.random.key(seed)
        x = -0.000125 + 0.9999 * jax.random.normal(jax.random.fold_in(_rk, 1), (128, 32, 512), jnp.float32)
        _lenS = 32 - jax.random.randint(jax.random.fold_in(_rk, 7), (128,), 0, max(1, 32 // 4) + 1, jnp.int32)
        _lenS2 = 32 - jax.random.randint(jax.random.fold_in(_rk, 8), (128,), 0, max(1, 32 // 4) + 1, jnp.int32)
        cond_128 = 0.0061147 + 1.02565 * jax.random.normal(jax.random.fold_in(_rk, 11), (128, 128), jnp.float32)
        fside_S_0 = -0.022604 + 0.987366 * jax.random.normal(jax.random.fold_in(_rk, 12), (32,), jnp.float32)
        return (x, cond_128, fside_S_0)
    x, cond_128, fside_S_0 = _rec_inputs()

    def _L0_cond_setup():
        import jax, jax.numpy as jnp
        import numpy as np
        K = 8
        T = 1.0
        D_EMBD = 128
        IN_C = 32
        OUT_C = 32
        BS = 32
        H = 512
        HID = 128
        key = jax.random.key(seed)
        ks = jax.random.split(key, 10)
        s = lambda fan_in: 1.0 / np.sqrt(fan_in)
        return {'x': jax.random.normal(ks[0], (BS, IN_C, H), dtype=jnp.float32), 'embedding': jax.random.normal(ks[1], (BS, D_EMBD), dtype=jnp.float32), 'W0': jax.random.normal(ks[2], (D_EMBD, HID), dtype=jnp.float32) * s(D_EMBD), 'b0': jnp.zeros((HID,), dtype=jnp.float32), 'W1': jax.random.normal(ks[3], (HID, HID), dtype=jnp.float32) * s(HID), 'b1': jnp.zeros((HID,), dtype=jnp.float32), 'W2': jax.random.normal(ks[4], (HID, K), dtype=jnp.float32) * s(HID), 'b2': jnp.zeros((K,), dtype=jnp.float32), 'weight': jax.random.normal(ks[5], (K, OUT_C, IN_C, 1), dtype=jnp.float32) * s(IN_C), 'bias_k': jax.random.normal(ks[6], (K, OUT_C), dtype=jnp.float32) * 0.1}
    _L0_cond_all = _L0_cond_setup()
    _L0_cond_in = {k: v for k, v in _L0_cond_all.items() if k in ('W0', 'b0', 'W1', 'b1', 'W2', 'b2', 'weight', 'bias_k')}
    del _L0_cond_all

    def _L0_attn_setup():
        import jax, jax.numpy as jnp
        import numpy as np
        NEG_INF = -1e+30

        def rotary_pos_emb(x):
            B, T, H, D = x.shape
            exponents = (jnp.arange(0, D, 2)[:D // 2] // D).astype(jnp.float32)
            freqs = 1.0 / jnp.power(jnp.float32(1000.0), exponents)
            theta = jnp.arange(T, dtype=jnp.float32)[:, None] * freqs[None, :]
            cos = jnp.cos(theta)[None, :, None, :]
            sin = jnp.sin(theta)[None, :, None, :]
            xr = x.astype(jnp.float32).reshape(B, T, H, D // 2, 2)
            x0, x1 = (xr[..., 0], xr[..., 1])
            out = jnp.stack([x0 * cos - x1 * sin, x0 * sin + x1 * cos], axis=-1)
            return out.reshape(B, T, H, D).astype(x.dtype)

        def attention_fwd(x, wq, wk, wv, wo, n_heads=32):
            B, T, C = x.shape
            hd = C // n_heads
            xq = (x @ wq.T).reshape(B, T, n_heads, hd)
            xk = (x @ wk.T).reshape(B, T, n_heads, hd)
            xv = (x @ wv.T).reshape(B, T, n_heads, hd)
            xq = rotary_pos_emb(xq)
            xk = rotary_pos_emb(xk)
            scale = hd ** (-0.5)
            scores = jnp.einsum('bqhd,bkhd->bhqk', xq, xk) * scale
            causal = jnp.tril(jnp.ones((T, T), dtype=bool))
            scores = jnp.where(causal[None, None], scores, NEG_INF)
            probs = jax.nn.softmax(scores.astype(jnp.float32), axis=-1).astype(xq.dtype)
            out = jnp.einsum('bhqk,bkhd->bqhd', probs, xv).reshape(B, T, C)
            return out @ wo.T
        key = jax.random.key(seed)
        ks = jax.random.split(key, 5)
        B, T, C = (2, 256, 512)
        s = 0.02
        return {'x': jax.random.normal(ks[0], (B, T, C), jnp.float32), 'wq': jax.random.normal(ks[1], (C, C), jnp.float32) * s, 'wk': jax.random.normal(ks[2], (C, C), jnp.float32) * s, 'wv': jax.random.normal(ks[3], (C, C), jnp.float32) * s, 'wo': jax.random.normal(ks[4], (C, C), jnp.float32) * s}
    _L0_attn_all = _L0_attn_setup()
    _L0_attn_in = {k: v for k, v in _L0_attn_all.items() if k in ('wq', 'wk', 'wv', 'wo')}
    del _L0_attn_all

    def _L0_cond2_setup():
        import jax, jax.numpy as jnp
        import numpy as np
        from jax import lax
        N, C_IN, L = (32, 32, 512)
        C_OUT, K, GROUPS = (32, 9, 4)
        C_DIM, PAD, STRIDE = (128, 4, 1)
        key = jax.random.key(seed)
        k1, k2, k3, k4, k5 = jax.random.split(key, 5)
        x = jax.random.normal(k1, (N, C_IN, L), dtype=jnp.float32)
        c = jax.random.normal(k2, (N, C_DIM), dtype=jnp.float32)
        weight = jax.random.normal(k3, (C_OUT, C_IN // GROUPS, K), dtype=jnp.float32)
        c_weight = jax.random.normal(k4, (C_OUT, C_DIM), dtype=jnp.float32)
        bias = jax.random.normal(k5, (C_OUT,), dtype=jnp.float32)
        return {'x': x, 'c': c, 'weight': weight, 'c_weight': c_weight, 'bias': bias}
    _L0_cond2_all = _L0_cond2_setup()
    _L0_cond2_in = {k: v for k, v in _L0_cond2_all.items() if k in ('weight', 'c_weight')}
    del _L0_cond2_all

    def _L0_ffn_setup():
        import jax, jax.numpy as jnp
        import numpy as np
        BATCH, TOK, DIM, OUT = (4, 256, 512, 512)
        E, R, TOP_K = (8, 16, 2)
        SCALING = 16.0 / R
        key = jax.random.key(seed)
        ks = jax.random.split(key, 6)
        return {'x': jax.random.normal(ks[0], (BATCH, TOK, DIM), dtype=jnp.float32), 'W_base': jax.random.normal(ks[1], (OUT, DIM), dtype=jnp.float32) / np.sqrt(DIM), 'b_base': jax.random.normal(ks[2], (OUT,), dtype=jnp.float32) * 0.01, 'W_gate': jax.random.normal(ks[3], (E, DIM), dtype=jnp.float32) * 0.01, 'A': jax.random.normal(ks[4], (E, R, DIM), dtype=jnp.float32) / np.sqrt(DIM), 'B': jax.random.normal(ks[5], (OUT, OUT // OUT * R * 0 + R), dtype=jnp.float32)[None].repeat(E, 0) * 0.0 + jax.random.normal(ks[5], (E, OUT, R), dtype=jnp.float32) * 0.02}
    _L0_ffn_all = _L0_ffn_setup()
    _L0_ffn_in = {k: v for k, v in _L0_ffn_all.items() if k in ('W_base', 'b_base', 'W_gate', 'A', 'B')}
    del _L0_ffn_all
    return {'x': x, 'cond_128': cond_128, 'fside_S_0': fside_S_0, 'L0_cond_W0': _L0_cond_in['W0'], 'L0_cond_b0': _L0_cond_in['b0'], 'L0_cond_W1': _L0_cond_in['W1'], 'L0_cond_b1': _L0_cond_in['b1'], 'L0_cond_W2': _L0_cond_in['W2'], 'L0_cond_b2': _L0_cond_in['b2'], 'L0_cond_weight': _L0_cond_in['weight'], 'L0_cond_bias_k': _L0_cond_in['bias_k'], 'L0_attn_wq': _L0_attn_in['wq'], 'L0_attn_wk': _L0_attn_in['wk'], 'L0_attn_wv': _L0_attn_in['wv'], 'L0_attn_wo': _L0_attn_in['wo'], 'L0_cond2_weight': _L0_cond2_in['weight'], 'L0_cond2_c_weight': _L0_cond2_in['c_weight'], 'L0_ffn_W_base': _L0_ffn_in['W_base'], 'L0_ffn_b_base': _L0_ffn_in['b_base'], 'L0_ffn_W_gate': _L0_ffn_in['W_gate'], 'L0_ffn_A': _L0_ffn_in['A'], 'L0_ffn_B': _L0_ffn_in['B']}

def reference(x, cond_128, fside_S_0, L0_cond_W0, L0_cond_b0, L0_cond_W1, L0_cond_b1, L0_cond_W2, L0_cond_b2, L0_cond_weight, L0_cond_bias_k, L0_attn_wq, L0_attn_wk, L0_attn_wv, L0_attn_wo, L0_cond2_weight, L0_cond2_c_weight, L0_ffn_W_base, L0_ffn_b_base, L0_ffn_W_gate, L0_ffn_A, L0_ffn_B):
    import jax
    import jax.numpy as jnp

    def _L0_cond_ref(x, embedding, W0, b0, W1, b1, W2, b2, weight, bias_k):
        import jax, jax.numpy as jnp
        import numpy as np
        K = 8
        T = 1.0
        D_EMBD = 128
        IN_C = 32
        OUT_C = 32
        BS = 32
        H = 512
        HID = 128
        h = jax.nn.gelu(embedding @ W0 + b0, approximate=False)
        h = jax.nn.gelu(h @ W1 + b1, approximate=False)
        att = jax.nn.softmax((h @ W2 + b2) / T, axis=-1)
        agg_w = jnp.einsum('bk,koi->boi', att, weight[..., 0])
        agg_b = att @ bias_k
        out = jnp.einsum('boi,bih->boh', agg_w, x) + agg_b[:, :, None]
        return out

    def _L0_attn_ref(x, wq, wk, wv, wo):
        import jax, jax.numpy as jnp
        import numpy as np
        NEG_INF = -1e+30

        def rotary_pos_emb(x):
            B, T, H, D = x.shape
            exponents = (jnp.arange(0, D, 2)[:D // 2] // D).astype(jnp.float32)
            freqs = 1.0 / jnp.power(jnp.float32(1000.0), exponents)
            theta = jnp.arange(T, dtype=jnp.float32)[:, None] * freqs[None, :]
            cos = jnp.cos(theta)[None, :, None, :]
            sin = jnp.sin(theta)[None, :, None, :]
            xr = x.astype(jnp.float32).reshape(B, T, H, D // 2, 2)
            x0, x1 = (xr[..., 0], xr[..., 1])
            out = jnp.stack([x0 * cos - x1 * sin, x0 * sin + x1 * cos], axis=-1)
            return out.reshape(B, T, H, D).astype(x.dtype)

        def attention_fwd(x, wq, wk, wv, wo, n_heads=32):
            B, T, C = x.shape
            hd = C // n_heads
            xq = (x @ wq.T).reshape(B, T, n_heads, hd)
            xk = (x @ wk.T).reshape(B, T, n_heads, hd)
            xv = (x @ wv.T).reshape(B, T, n_heads, hd)
            xq = rotary_pos_emb(xq)
            xk = rotary_pos_emb(xk)
            scale = hd ** (-0.5)
            scores = jnp.einsum('bqhd,bkhd->bhqk', xq, xk) * scale
            causal = jnp.tril(jnp.ones((T, T), dtype=bool))
            scores = jnp.where(causal[None, None], scores, NEG_INF)
            probs = jax.nn.softmax(scores.astype(jnp.float32), axis=-1).astype(xq.dtype)
            out = jnp.einsum('bhqk,bkhd->bqhd', probs, xv).reshape(B, T, C)
            return out @ wo.T
        return attention_fwd(x, wq, wk, wv, wo)

    def _L0_cond2_ref(x, c, weight, c_weight, bias):
        import jax, jax.numpy as jnp
        import numpy as np
        from jax import lax
        N, C_IN, L = (32, 32, 512)
        C_OUT, K, GROUPS = (32, 9, 4)
        C_DIM, PAD, STRIDE = (128, 4, 1)
        out = lax.conv_general_dilated(x, weight, window_strides=(STRIDE,), padding=[(PAD, PAD)], dimension_numbers=('NCH', 'OIH', 'NCH'), feature_group_count=GROUPS)
        ctx = jnp.einsum('nd,od->no', c, c_weight)
        out = out + ctx[:, :, None] + bias[None, :, None]
        return out

    def _L0_ffn_ref(x, W_base, b_base, W_gate, A, B):
        import jax, jax.numpy as jnp
        import numpy as np
        BATCH, TOK, DIM, OUT = (4, 256, 512, 512)
        E, R, TOP_K = (8, 16, 2)
        SCALING = 16.0 / R
        result = jnp.einsum('bnd,od->bno', x, W_base) + b_base
        logits = jnp.einsum('bnd,ed->bne', x, W_gate)
        probs = jax.nn.softmax(logits.astype(jnp.float32), axis=-1)
        top_p, top_i = jax.lax.top_k(probs, TOP_K)
        top_p = top_p / jnp.sum(top_p, axis=-1, keepdims=True)
        top_p = top_p.astype(x.dtype)
        route_w = jnp.sum(jax.nn.one_hot(top_i, E, dtype=x.dtype) * top_p[..., None], axis=-2)
        h = jnp.einsum('bnd,erd->bner', x, A)
        hw = h * route_w[..., None]
        delta = jnp.einsum('bner,eor->bno', hw, B)
        return result + delta * SCALING
    x = x + _L0_attn_ref(_L0_cond_ref(x, cond_128, L0_cond_W0, L0_cond_b0, L0_cond_W1, L0_cond_b1, L0_cond_W2, L0_cond_b2, L0_cond_weight, L0_cond_bias_k), L0_attn_wq, L0_attn_wk, L0_attn_wv, L0_attn_wo)
    x = x + _L0_ffn_ref(_L0_cond2_ref(x, cond_128, L0_cond2_weight, L0_cond2_c_weight, fside_S_0), L0_ffn_W_base, L0_ffn_b_base, L0_ffn_W_gate, L0_ffn_A, L0_ffn_B)
    return x

_drawn_inputs = setup_inputs


def setup_inputs(seed=0):
    import zlib

    import numpy as np

    out = dict(_drawn_inputs(seed))
    spreads = {'L0_cond_b0': (0.0, 0.8), 'L0_cond_b1': (0.0, 0.8), 'L0_cond_b2': (0.0, 2.0)}
    factors = {'L0_cond_W0': 8.0,
     'L0_cond_W1': 8.0,
     'L0_cond_W2': 8.0,
     'L0_cond_weight': 3.137,
     'L0_cond_bias_k': 8.0,
     'L0_attn_wq': 8.0,
     'L0_attn_wk': 8.0,
     'L0_attn_wv': 3.464,
     'L0_attn_wo': 3.451,
     'L0_ffn_b_base': 200.0,
     'fside_S_0': 4.796}
    for name, (base, spread) in spreads.items():
        noise = np.random.default_rng([zlib.crc32(name.encode()), seed]).standard_normal(out[name].shape)
        drawn = base * np.exp(spread * noise) if base else spread * noise
        out[name] = jnp.asarray(drawn.astype(out[name].dtype))
    for name, factor in factors.items():
        out[name] = (out[name] * factor).astype(out[name].dtype)
    return out
```

```python
import numpy as np
import concourse.bass as bass
from concourse import mybir
from contextlib import ExitStack

F32 = mybir.dt.float32
F32R = mybir.dt.float32r
BF16 = mybir.dt.bfloat16
U32 = mybir.dt.uint32
ALU = mybir.AluOpType
ACT = mybir.ActivationFunctionType
AX = mybir.AxisListType

P = 128
B, T, C = 128, 32, 512
H, HD = 32, 16
BPT = P // T
NT = B // BPT
TPM = 4
NM = NT // TPM
CK = C // P
MCOL = TPM * P
NE, RANK = 8, 16
NA = NE * RANK
NG = NA + NE
TAPS, PAD = 9, 4
SH = 3
XW = C + 2 * PAD
BANK = 512

C_ID, C_ROT, C_KM, C_IO, C_MASK = 0, 128, 134, 138, 146
NC = C_MASK + C


def build(nc, io):
    ctx = ExitStack()
    with ctx:
        def sb(name, shape, dt=F32):
            return ctx.enter_context(nc.sbuf_tensor(name, shape, dt))

        def sem(name):
            return ctx.enter_context(nc.semaphore(name))

        names = ["wq", "wk", "wv", "wo", "wb"]
        w_hi = {n: sb(n + "_hi", [P, CK, C], F32R) for n in names}
        w_lo = {n: sb(n + "_lo", [P, CK, C], F32R) for n in names}
        const = sb("const", [P, NC])
        maskb = sb("maskb", [P, C], BF16)
        identb = sb("identb", [P, P], BF16)
        ones = sb("ones", [P, P])
        wag = sb("wag", [P, CK, NG])
        wbt = sb("wbt", [P, C])
        wconv = sb("wconv", [SH * T, TAPS // SH, T])
        bbase = sb("bbase", [P, C])
        mixT = sb("mixT", [P, NT, P])
        cbias = sb("cbias", [P, NT])
        xst = sb("xst", [P, CK, C])
        aggb = sb("aggb", [P, T])
        xin = sb("xin", [P, TPM, C])
        x1 = sb("x1", [P, C])
        x1b = sb("x1b", [P, 2, C])
        x3 = sb("x3", [SH * T, BPT, XW])
        aggbc = sb("aggbc", [P, MCOL])
        xdiag = sb("xdiag", [P, MCOL])
        yf = sb("yf", [P, CK, P])
        yhi = sb("yhi", [P, CK, P], F32R)
        ylo = sb("ylo", [P, CK, P], F32R)
        qr = sb("qr", [P, C])
        kr = sb("kr", [P, C])
        qT = sb("qT", [P, CK, P])
        kT = sb("kT", [P, CK, P])
        kbd = sb("kbd", [P, CK, 4, P])
        vsb = sb("vsb", [P, 4, P])
        vbd = sb("vbd", [P, BPT, 4, P])
        es = sb("es", [P, H * T])
        pT = sb("pT", [P, H // 4, P])
        onat = sb("onat", [P, C])
        ohi = sb("ohi", [P, CK, P], F32R)
        olo = sb("olo", [P, CK, P], F32R)
        zsb = sb("zsb", [P, C])
        zTf = sb("zTf", [P, CK, P])
        zhi = sb("zhi", [P, CK, P], F32R)
        zlo = sb("zlo", [P, CK, P], F32R)
        zbias = sb("zbias", [P, 1])
        ost = sb("ost", [P, C])
        hw = sb("hw", [P, NA])
        hwT = sb("hwT", [P, NA])
        rmx = sb("rmx", [P, H])
        rsum = sb("rsum", [P, H])
        rinv = sb("rinv", [P, H])
        r8 = sb("r8", [P, 72])
        ri = sb("ri", [P, 8], U32)

        ps = ctx.enter_context(nc.psum_tensor("ps", [P, 8 * BANK], F32))

        def bank(n, width=1):
            return ps[:, n * BANK:(n + width) * BANK]

        condT = kr[:, 0:B]
        W0, W1 = es[:, 0:128], es[:, 128:256]
        h1, h2 = es[:, 256:384], es[:, 384:512]
        W2 = es[:, 512:520]
        small = es[:, 520:600]
        cwsb = pT[:, :, :].rearrange("p a b -> p (a b)")[0:8, 0:T * T]
        attT = qr[0:8, 0:B]
        biask = qr[0:8, 128:160]
        cwT = kr[:, 128:128 + T]
        fside = kr[:, 160:161]
        stage = [t[:, :, :, :].rearrange("p a b c -> p a (b c)") for t in (kbd, vbd)] + [xst[:, :, :]]
        staged = {"wq": stage[0], "wk": stage[1], "wv": stage[2], "wo": stage[0], "wb": stage[2]}

        ident = const[:, C_ID:C_ID + P]
        rot = const[:, C_ROT:C_ROT + 6]
        kmask = const[:, C_KM:C_KM + 4]
        iota8 = const[:, C_IO:C_IO + 8]

        ld_cond, ld_const, ld_misc = sem("ld_cond"), sem("ld_const"), sem("ld_misc")
        ld_w = {n: sem("ld_" + n) for n in names}
        ld_x = [sem(f"ld_x{j}") for j in range(TPM)]
        whi_done = {n: sem(f"whi_{n}") for n in names}
        wlo_done = {n: sem(f"wlo_{n}") for n in names}
        zeroed, su_pe, su_act, su_dve = sem("zeroed"), sem("su_pe"), sem("su_act"), sem("su_dve")
        bc_d, bc_ps, bc_sb = sem("bc_d"), sem("bc_ps"), sem("bc_sb")
        cond_ps, y_f, y_hi, y_lo = sem("cond_ps"), sem("y_f"), sem("y_hi"), sem("y_lo")
        q_ps, k_ps, v_ps = sem("q_ps"), sem("k_ps"), sem("v_ps")
        q_cos, k_cos, v_sb, v_bd = sem("q_cos"), sem("k_cos"), sem("v_sb"), sem("v_bd")
        q_rot, k_rot = sem("q_rot"), sem("k_rot")
        tq_ps, tk_ps, qT_sb, kT_sb = sem("tq_ps"), sem("tk_ps"), sem("qT_sb"), sem("kT_sb")
        kbd_v, kbd_g = sem("kbd_v"), sem("kbd_g")
        s_ps, s_max, s_sub, s_exp, s_sum, s_inv, p_norm = (
            sem("s_ps"), sem("s_max"), sem("s_sub"), sem("s_exp"), sem("s_sum"), sem("s_inv"), sem("p_norm"))
        pt_ps, pT_a, pT_v, pv_ps, o_sb = sem("pt_ps"), sem("pT_a"), sem("pT_v"), sem("pv_ps"), sem("o_sb")
        to_ps, o_hi, o_lo, wo_ps = sem("to_ps"), sem("o_hi"), sem("o_lo"), sem("wo_ps")
        x1_sb, x1b_sb, x3_sb = sem("x1_sb"), sem("x1b_sb"), sem("x3_sb")
        conv_ps, zb_sb, z_sb = sem("conv_ps"), sem("zb_sb"), sem("z_sb")
        tz_ps, z_f, z_hi, z_lo = sem("tz_ps"), sem("z_f"), sem("z_hi"), sem("z_lo")
        ag_ps, r_top, r_sub, r_exp, r_step, hw_sb = (
            sem("ag_ps"), sem("r_top"), sem("r_sub"), sem("r_exp"), sem("r_step"), sem("hw_sb"))
        ht_ps, hwT_sb, f_ps, f_out, stored = (
            sem("ht_ps"), sem("hwT_sb"), sem("f_ps"), sem("f_out"), sem("stored"))

        def need(eng, s, value):
            if isinstance(value, int) and value <= 0:
                return
            eng.wait_ge(s, value)

        def at(t, n=P):
            return slice(t * n, t * n + n) if isinstance(t, int) else bass.ds(t * n, n)

        def rows(eng, t):
            return at(t) if isinstance(t, int) else bass.ds(eng.snap(t * P), P)

        def run_slots(eng, slot):
            def four(m, first=False, last=False):
                for j in range(TPM):
                    slot(TPM * m + j, m, j, cur=True, prev=not (first and j == 0),
                         nxt=not (last and j == TPM - 1), ffn=not (first and j < 2))
            four(0, first=True)
            with eng.Fori(1, NM - 1) as m:
                four(m)
            four(NM - 1, last=True)
            slot(NT, NM, 0, cur=False, prev=True, nxt=False, ffn=True)
            slot(NT + 1, NM, 1, cur=False, prev=False, nxt=False, ffn=True)

        block = ctx.enter_context(nc.Block())

        @block.sync
        def _(sp):
            for dst, name in ((condT, "condT"), (W0, "W0"), (small[:, 0:1], "b0"), (W1, "W1"),
                              (small[:, 1:2], "b1"), (W2, "W2")):
                sp.dma_start(dst, io[name]).then_inc(ld_cond, 16)
            sp.dma_start(small[:, 8:16], io["b2"].to_broadcast([P, NE])).then_inc(ld_cond, 16)
            sp.dma_start(cwsb, io["cw"]).then_inc(ld_cond, 16)
            sp.dma_start(biask, io["biask"]).then_inc(ld_cond, 16)
            sp.dma_start(cwT, io["cwT"]).then_inc(ld_cond, 16)
            sp.dma_start(fside, io["fside"]).then_inc(ld_cond, 16)
            sp.dma_start(xin[:, 0, :], io["x"][0:P, :]).then_inc(ld_x[0], 16)
            for n in ("wq", "wk", "wv"):
                sp.dma_start(staged[n], io[n]).then_inc(ld_w[n], 16)
            for j in range(1, TPM):
                sp.dma_start(xin[:, j, :], io["x"][at(j), :]).then_inc(ld_x[j], 16)
            sp.dma_start(wconv[:, :, :], io["wconv"]).then_inc(ld_misc, 16)
            sp.dma_start(wag[:, :, 0:NA], io["wa"]).then_inc(ld_misc, 16)
            sp.dma_start(wag[:, :, NA:NG], io["wg"]).then_inc(ld_misc, 16)
            sp.dma_start(wbt[:, :], io["wbt"]).then_inc(ld_misc, 16)
            sp.dma_start(bbase[:, :], io["bbase"].to_broadcast([P, C])).then_inc(ld_misc, 16)
            for n, before in (("wo", "wq"), ("wb", "wv")):
                sp.wait_ge(whi_done[before], 1)
                sp.wait_ge(wlo_done[before], 1)
                sp.dma_start(staged[n], io[n]).then_inc(ld_w[n], 16)

            def slot(t, m, j, cur, prev, nxt, ffn):
                more = prev and not (isinstance(t, int) and t + TPM - 1 >= NT)
                x_rows = rows(sp, t + TPM - 1) if more else None
                out_rows = rows(sp, t - 2) if ffn else None
                if cur:
                    sp.wait_ge(v_sb, t + 1)
                    need(sp, pv_ps, t)
                    if isinstance(t, int) and t == 0:
                        sp.wait_ge(zeroed, 4)
                    for h in range(4):
                        for b in range(BPT):
                            sp.dma_start(vbd[32 * h:32 * h + 32, b, h, :],
                                         vsb[32 * b:32 * b + 32, h, :]).then_inc(v_bd, 16)
                if prev:
                    sp.wait_ge(x1_sb, t)
                    for s_ in range(SH):
                        for b in range(BPT):
                            sp.dma_start(x3[32 * s_:32 * s_ + 32, b, PAD - s_:PAD - s_ + C],
                                         x1[32 * b:32 * b + 32, :]).then_inc(x3_sb, 16)
                    if more:
                        jn = (j - 1) % TPM
                        sp.dma_start(xin[:, jn, :], io["x"][x_rows, :]).then_inc(ld_x[jn], 16)
                if ffn:
                    sp.wait_ge(f_out, t - 1)
                    sp.dma_start(io["out"][out_rows, :], ost[:, :]).then_inc(stored, 16)

            run_slots(sp, slot)
            sp.wait_ge(stored, 16 * NT)

        @block.tensor
        def _(pe):
            def split_mm(out, hi, lo, name, last=True):
                parts = ((hi, w_hi[name]), (hi, w_lo[name]), (lo, w_hi[name]))
                for a, (x, w) in enumerate(parts):
                    for c in range(CK):
                        mm = pe.matmul(out, x[:, c, :], w[:, c, :], start=(a == 0 and c == 0),
                                       stop=(last and a == 2 and c == CK - 1), skip_group_check=True)
                return mm

            def turn(n, src, done):
                for c in range(CK):
                    mm = pe.transpose(bank(n)[:, c * P:(c + 1) * P], src[:, c * P:(c + 1) * P], ident)
                mm.then_inc(done, 1)

            def broadcast_bias(m, first=False):
                pe.wait_ge(bc_d, m + 1)
                if not first:
                    pe.wait_ge(x1_sb, TPM * m - 2)
                pe.matmul(bank(7), ones[:, :], xdiag[:, :], start=True, stop=True).then_inc(bc_ps, 1)

            def mix(t, m, j):
                pe.wait_ge(ld_x[j], 16 * (m + 1))
                mixing = mixT[:, t, :] if isinstance(t, int) else \
                    mixT[:, bass.ds(t, 1), :].rearrange("p o c -> p (o c)")
                for c in range(CK):
                    mm = pe.matmul(bank(7)[:, c * P:(c + 1) * P], xin[:, j, c * P:(c + 1) * P], mixing,
                                   start=True, stop=True, skip_group_check=True)
                mm.then_inc(cond_ps, 1)

            def slot(t, m, j, cur, prev, nxt, ffn):
                if cur:
                    pe.wait_ge(y_hi, t + 1)
                    pe.wait_ge(y_lo, t + 1)
                    need(pe, o_lo, t - 1)
                    split_mm(bank(6), yhi, ylo, "wq").then_inc(q_ps, 1)
                if cur:
                    need(pe, o_sb, t - 1)
                    split_mm(bank(4), yhi, ylo, "wk").then_inc(k_ps, 1)
                if cur:
                    need(pe, hwT_sb, t - 2)
                    split_mm(bank(5), yhi, ylo, "wv").then_inc(v_ps, 1)
                if nxt and j == TPM - 1:
                    broadcast_bias(m + 1)
                if prev:
                    pe.wait_ge(p_norm, t)
                    for g in range(H // 4):
                        mm = pe.transpose(bank(0, 2)[:, g * P:(g + 1) * P], es[:, g * P:(g + 1) * P], ident)
                    mm.then_inc(pt_ps, 1)
                if ffn:
                    pe.wait_ge(x3_sb, 16 * SH * BPT * (t - 1))
                    if cur:
                        pe.wait_ge(q_rot, t + 1)
                    for g in range(TAPS // SH):
                        for b in range(BPT):
                            mm = pe.matmul(bank(6)[32 * b:32 * b + 32, :], wconv[:, g, :],
                                           x3[:, b, SH * g:SH * g + C], start=(g == 0),
                                           stop=(g == TAPS // SH - 1), skip_group_check=True)
                    mm.then_inc(conv_ps, 1)
                if cur:
                    pe.wait_ge(q_rot, t + 1)
                    need(pe, f_out, t - 2)
                    turn(2, qr, tq_ps)
                    pe.wait_ge(k_rot, t + 1)
                    turn(3, kr, tk_ps)
                if nxt:
                    need(pe, x1_sb, t - 1)
                    if j == TPM - 1:
                        pe.wait_ge(bc_sb, m + 2)
                    mix(t + 1, m + (j + 1) // TPM, (j + 1) % TPM)
                if prev:
                    pe.wait_ge(pT_a, t)
                    pe.wait_ge(pT_v, t)
                    pe.wait_ge(v_bd, 16 * 4 * BPT * t)
                    if cur:
                        pe.wait_ge(k_rot, t + 1)
                    for g in range(H // 4):
                        for b in range(BPT):
                            mm = pe.matmul(bank(4)[32 * b:32 * b + 32, g * 64:(g + 1) * 64],
                                           pT[:, g, 32 * b:32 * b + 32], vbd[:, b, :, g * HD:(g + 1) * HD],
                                           start=True, stop=True, skip_group_check=True)
                    mm.then_inc(pv_ps, 1)
                if ffn:
                    pe.wait_ge(z_sb, t - 1)
                    if cur:
                        pe.wait_ge(v_sb, t + 1)
                    turn(5, zsb, tz_ps)
                if prev:
                    pe.wait_ge(o_sb, t)
                    need(pe, z_sb, t - 1)
                    turn(6, onat, to_ps)
                if cur:
                    pe.wait_ge(qT_sb, t + 1)
                    pe.wait_ge(kbd_v, t + 1)
                    pe.wait_ge(kbd_g, t + 1)
                    for n in range(2):
                        pe.matmul(bank(n), identb[:, :], maskb[:, :], start=True, stop=False,
                                  skip_group_check=True)
                    for c in range(CK):
                        for g in range(2):
                            for b in range(BPT):
                                mm = pe.matmul(
                                    bank(g)[32 * b:32 * b + 32, c * P:(c + 1) * P],
                                    qT[64 * g:64 * g + 64, c, 32 * b:32 * b + 32],
                                    kbd[64 * g:64 * g + 64, c, :, 32 * b:32 * b + 32],
                                    start=False, stop=(c == CK - 1), skip_group_check=True)
                    mm.then_inc(s_ps, 1)
                if ffn:
                    pe.wait_ge(z_f, t - 1)
                    for c in range(CK):
                        mm = pe.matmul(bank(5)[:, 0:NG], zTf[:, c, :], wag[:, c, :],
                                       start=(c == 0), stop=(c == CK - 1), skip_group_check=True)
                    mm.then_inc(ag_ps, 1)
                if prev:
                    pe.wait_ge(o_hi, t)
                    pe.wait_ge(o_lo, t)
                    if nxt:
                        pe.wait_ge(y_f, t + 2)
                    split_mm(bank(7), ohi, olo, "wo").then_inc(wo_ps, 1)
                if ffn:
                    pe.wait_ge(z_hi, t - 1)
                    pe.wait_ge(z_lo, t - 1)
                    if cur:
                        pe.wait_ge(qT_sb, t + 1)
                    split_mm(bank(2), zhi, zlo, "wb", last=False)
                    pe.wait_ge(hw_sb, t - 1)
                    pe.transpose(bank(5)[:, 256:256 + NA], hw[:, :], ident).then_inc(ht_ps, 1)
                    pe.wait_ge(hwT_sb, t - 1)
                    pe.matmul(bank(2), hwT[:, :], wbt[:, :], start=False, stop=True,
                              skip_group_check=True).then_inc(f_ps, 1)

            pe.wait_ge(ld_cond, 16 * 11)
            pe.matmul(bank(0)[:, 0:P], W0, condT, start=True, stop=True).then_inc(su_pe, 1)
            pe.wait_ge(su_act, 1)
            pe.matmul(bank(1)[:, 0:P], W1, h1, start=True, stop=True).then_inc(su_pe, 1)
            pe.wait_ge(su_act, 2)
            pe.matmul(bank(2)[:, 0:NE], h2, W2, start=True, stop=True).then_inc(su_pe, 1)
            condv = condT.rearrange("d (s r) -> d r s", r=BPT)
            for r in range(BPT):
                mm = pe.matmul(bank(6)[32 * r:32 * r + 32, 0:NT], cwT, condv[:, r, :],
                               start=True, stop=True, skip_group_check=True)
            mm.then_inc(su_pe, 1)
            pe.wait_ge(su_dve, 6)
            pe.wait_ge(ld_const, 16)
            pe.transpose(bank(3)[0:NE, 0:P], small[:, 24:32], ident).then_inc(su_pe, 1)
            pe.wait_ge(su_dve, 7)
            pe.matmul(bank(2)[:, 16:16 + T], attT, biask, start=True, stop=True).then_inc(su_pe, 1)
            cwv = cwsb.rearrange("k (o i) -> k o i", i=T)
            attv = attT.rearrange("k (s r) -> k r s", r=BPT)
            for o in range(T):
                for r in range(BPT):
                    mm = pe.matmul(bank(4, 2)[32 * r:32 * r + 32, o * NT:(o + 1) * NT], cwv[:, o, :], attv[:, r, :],
                                   start=True, stop=True, skip_group_check=True)
            mm.then_inc(su_pe, 1)
            broadcast_bias(0, first=True)
            pe.wait_ge(bc_sb, 1)
            pe.wait_ge(su_act, 5)
            mix(0, 0, 0)
            for n in names:
                pe.wait_ge(whi_done[n], 1)
                pe.wait_ge(wlo_done[n], 1)
            pe.wait_ge(ld_misc, 16 * 5)
            pe.wait_ge(su_dve, 11)
            pe.wait_ge(zeroed, 4)
            run_slots(pe, slot)

        @block.scalar
        def _(act):
            def y_high(t):
                act.wait_ge(y_f, t + 1)
                need(act, v_ps, t)
                act.copy(yhi[:, :, :], yf[:, :, :]).then_inc(y_hi, 1)

            def four(n):
                return bank(n).rearrange("p (c r) -> p c r", c=CK)

            def slot(t, m, j, cur, prev, nxt, ffn):
                if cur:
                    act.wait_ge(q_ps, t + 1)
                    need(act, tq_ps, t)
                    act.activation(qr[:, :], bank(6), ACT.Copy, scale=rot[:, 0:1]).then_inc(q_cos, 1)
                if cur:
                    act.wait_ge(k_ps, t + 1)
                    need(act, tk_ps, t)
                    act.activation(kr[:, :], bank(4), ACT.Copy, scale=rot[:, 3:4]).then_inc(k_cos, 1)
                if cur:
                    act.wait_ge(v_ps, t + 1)
                    need(act, v_bd, 16 * 4 * BPT * t)
                    act.copy(vsb[:, :, :], four(5)).then_inc(v_sb, 1)
                if prev:
                    act.wait_ge(pt_ps, t)
                    need(act, pv_ps, t - 1)
                    act.copy(pT[:, 0:4, :], four(0)).then_inc(pT_a, 1)
                if ffn:
                    act.wait_ge(conv_ps, t - 1)
                    act.wait_ge(zb_sb, t - 1)
                    need(act, tz_ps, t - 2)
                    act.activation(zsb[:, :], bank(6), ACT.Identity, bias=zbias[:, 0:1]).then_inc(z_sb, 1)
                if cur:
                    act.wait_ge(tq_ps, t + 1)
                    need(act, s_ps, t)
                    act.copy(qT[:, :, :], four(2)).then_inc(qT_sb, 1)
                    act.wait_ge(tk_ps, t + 1)
                    need(act, kbd_v, t)
                    need(act, kbd_g, t)
                    act.copy(kT[:, :, :], four(3)).then_inc(kT_sb, 1)
                if nxt:
                    y_high(t + 1)
                if prev:
                    act.wait_ge(pv_ps, t)
                    need(act, to_ps, t - 1)
                    act.copy(onat[:, :], bank(4)).then_inc(o_sb, 1)
                if ffn:
                    act.wait_ge(tz_ps, t - 1)
                    need(act, ag_ps, t - 2)
                    need(act, z_lo, t - 2)
                    act.copy(zTf[:, :, :], four(5)).then_inc(z_f, 1)
                if prev:
                    act.wait_ge(to_ps, t)
                    need(act, wo_ps, t - 1)
                    act.copy(ohi[:, :, :], four(6)).then_inc(o_hi, 1)
                if cur:
                    act.wait_ge(s_sub, t + 1)
                    act.activation(es[:, :], es[:, :], ACT.Exp).then_inc(s_exp, 1)
                if ffn:
                    act.wait_ge(r_sub, t - 1)
                    act.activation(r8[:, 16:24], r8[:, 8:16], ACT.Exp).then_inc(r_exp, 1)
                    act.wait_ge(ht_ps, t - 1)
                    need(act, f_ps, t - 2)
                    act.copy(hwT[:, :], bank(5)[:, 256:256 + NA]).then_inc(hwT_sb, 1)

            act.dma_start(const[:, :], io["const"]).then_inc(ld_const, 16)
            act.wait_ge(ld_cond, 16 * 11)
            act.wait_ge(su_pe, 1)
            act.activation(h1, bank(0)[:, 0:P], ACT.Gelu, bias=small[:, 0:1]).then_inc(su_act, 1)
            act.wait_ge(su_pe, 2)
            act.activation(h2, bank(1)[:, 0:P], ACT.Gelu, bias=small[:, 1:2]).then_inc(su_act, 1)
            act.wait_ge(su_dve, 3)
            act.activation(small[:, 32:40], small[:, 16:24], ACT.Exp).then_inc(su_act, 1)
            for n in ("wq", "wk"):
                act.wait_ge(ld_w[n], 16)
                act.copy(w_hi[n][:, :, :], staged[n]).then_inc(whi_done[n], 1)
            act.wait_ge(su_pe, 7)
            act.wait_ge(zeroed, 1)
            for r in range(BPT):
                ins = act.copy(mixT[32 * r:32 * r + 32, :, 32 * r:32 * r + 32],
                               bank(4, 2)[32 * r:32 * r + 32, :].rearrange("i (o s) -> i s o", s=NT))
            ins.then_inc(su_act, 2)
            y_high(0)
            for n in ("wv", "wo", "wb"):
                act.wait_ge(ld_w[n], 16)
                act.copy(w_hi[n][:, :, :], staged[n]).then_inc(whi_done[n], 1)
            for n in names:
                act.wait_ge(wlo_done[n], 1)
            act.wait_ge(su_dve, 11)
            run_slots(act, slot)

        @block.vector
        def _(dve):
            def four(n):
                return bank(n).rearrange("p (c r) -> p c r", c=CK)

            def rotate(dst, src, k, done):
                d = dst[:, :].rearrange("p (h two e) -> p h two e", two=2, e=HD // 2)
                s = src.rearrange("p (h two e) -> p h two e", two=2, e=HD // 2)
                dve.scalar_tensor_tensor(out=d[:, :, 0, :], in0=s[:, :, 1, :], scalar=rot[:, k + 2:k + 3],
                                         in1=d[:, :, 0, :], op0=ALU.mult, op1=ALU.add)
                dve.scalar_tensor_tensor(out=d[:, :, 1, :], in0=s[:, :, 0, :], scalar=rot[:, k + 1:k + 2],
                                         in1=d[:, :, 1, :], op0=ALU.mult, op1=ALU.add).then_inc(done, 1)

            def lay_bias(m):
                need(dve, bc_ps, m)
                own = (const[:, C_ID + 16 * m:C_ID + 16 * m + 16] if isinstance(m, int) else
                       const[:, bass.ds(C_ID + 16 * m, 16)])
                dve.tensor_tensor(xdiag[:, :].rearrange("p (b t) -> p b t", t=T),
                                  aggb[:, None, :].to_broadcast([P, 16, T]),
                                  own[:, :, None].to_broadcast([P, 16, T]), ALU.mult).then_inc(bc_d, 1)

            def keep_bias(m):
                dve.wait_ge(bc_ps, m + 1)
                dve.tensor_copy(aggbc[:, :], bank(7)).then_inc(bc_sb, 1)

            def y_full(t, m, j):
                dve.wait_ge(cond_ps, t + 1)
                need(dve, y_hi, t)
                need(dve, y_lo, t)
                if j == 0:
                    dve.wait_ge(bc_sb, m + 1)
                dve.tensor_tensor(yf[:, :, :], four(7),
                                  aggbc[:, None, j * P:(j + 1) * P].to_broadcast([P, CK, P]),
                                  ALU.add).then_inc(y_f, 1)

            def route(t):
                f = t - 2
                dve.wait_ge(ag_ps, f + 1)
                dve.tensor_reduce(r8[:, 0:1], bank(5)[:, NA:NG], AX.X, ALU.max).then_inc(r_top, 1)
                dve.wait_ge(r_top, 2 * f + 1)
                need(dve, r_exp, f)
                dve.tensor_scalar(r8[:, 8:16], bank(5)[:, NA:NG], r8[:, 0:1], None,
                                  ALU.subtract).then_inc(r_sub, 1)

            def route_rest(t):
                f = t - 2
                dve.wait_ge(su_dve, 11)
                dve.wait_ge(r_exp, f + 1)
                dve.max(r8[:, 24:32], r8[:, 16:24]).then_inc(r_top, 1)
                dve.wait_ge(r_top, 2 * f + 2)
                dve.tensor_tensor(r8[:, 64:65], r8[:, 24:25], r8[:, 25:26], ALU.add).then_inc(r_step, 1)
                dve.max_index(ri[:, :], r8[:, 24:32], r8[:, 16:24]).then_inc(r_step, 1)
                dve.wait_ge(r_step, 6 * f + 2)
                dve.tensor_copy(r8[:, 32:40], ri[:, :]).then_inc(r_step, 1)
                dve.reciprocal(r8[:, 65:66], r8[:, 64:65])
                dve.wait_ge(r_step, 6 * f + 3)
                dve.tensor_scalar(r8[:, 40:48], iota8, r8[:, 32:33], r8[:, 24:25], ALU.is_equal,
                                  ALU.mult).then_inc(r_step, 1)
                dve.tensor_scalar(r8[:, 48:56], iota8, r8[:, 33:34], r8[:, 25:26], ALU.is_equal,
                                  ALU.mult).then_inc(r_step, 1)
                dve.wait_ge(r_step, 6 * f + 5)
                dve.tensor_tensor(r8[:, 56:64], r8[:, 40:48], r8[:, 48:56], ALU.add).then_inc(r_step, 1)
                dve.wait_ge(r_step, 6 * f + 6)
                need(dve, ht_ps, f)
                dve.scalar_tensor_tensor(out=hw[:, :].rearrange("p (e r) -> p e r", e=NE),
                                         in0=bank(5)[:, 0:NA].rearrange("p (e r) -> p e r", e=NE),
                                         scalar=r8[:, 65:66],
                                         in1=r8[:, 56:64, None].to_broadcast([P, NE, RANK]),
                                         op0=ALU.mult, op1=ALU.mult).then_inc(hw_sb, 1)

            def slot(t, m, j, cur, prev, nxt, ffn):
                if cur:
                    dve.wait_ge(q_cos, t + 1)
                    rotate(qr, bank(6), 0, q_rot)
                    dve.wait_ge(k_cos, t + 1)
                    rotate(kr, bank(4), 3, k_rot)
                if nxt and j == TPM - 1:
                    lay_bias(m + 1)
                    keep_bias(m + 1)
                if prev:
                    dve.wait_ge(pt_ps, t)
                    need(dve, pv_ps, t - 1)
                    dve.tensor_copy(pT[:, 4:8, :], four(1)).then_inc(pT_v, 1)
                if cur:
                    dve.wait_ge(kT_sb, t + 1)
                    need(dve, s_ps, t)
                    for h in range(3):
                        ins = dve.tensor_scalar(kbd[:, :, h, :], kT[:, :, :], kmask[:, h:h + 1], None, ALU.mult)
                    ins.then_inc(kbd_v, 1)
                if nxt:
                    y_full(t + 1, m + (j + 1) // TPM, (j + 1) % TPM)
                if ffn:
                    dve.wait_ge(z_f, t - 1)
                    need(dve, f_ps, t - 2)
                    dve.tensor_copy(zhi[:, :, :], zTf[:, :, :]).then_inc(z_hi, 1)
                if prev:
                    dve.wait_ge(o_hi, t)
                    need(dve, wo_ps, t - 1)
                    dve.tensor_tensor(olo[:, :, :], four(6), ohi[:, :, :].bitcast(F32),
                                      ALU.subtract).then_inc(o_lo, 1)
                if cur:
                    s3 = bank(0, 2).rearrange("p (h k) -> p h k", k=T)
                    e3 = es[:, :].rearrange("p (h k) -> p h k", k=T)
                    dve.wait_ge(s_ps, t + 1)
                    dve.tensor_reduce(rmx[:, :], s3, AX.X, ALU.max).then_inc(s_max, 1)
                    dve.wait_ge(s_max, t + 1)
                    need(dve, pt_ps, t)
                    dve.tensor_tensor(e3, s3, rmx[:, :, None].to_broadcast([P, H, T]),
                                      ALU.subtract).then_inc(s_sub, 1)
                if ffn:
                    route(t)
                    route_rest(t)
                if prev:
                    dve.wait_ge(wo_ps, t)
                    need(dve, x3_sb, 16 * SH * BPT * (t - 1))
                    need(dve, x1b_sb, t - 1)
                    dve.tensor_tensor(x1[:, :], bank(7), xin[:, (j - 1) % TPM, :],
                                      ALU.add).then_inc(x1_sb, 1)
                if cur:
                    dve.wait_ge(s_exp, t + 1)
                    dve.tensor_reduce(rsum[:, :], e3, AX.X, ALU.add).then_inc(s_sum, 1)
                    dve.wait_ge(s_sum, t + 1)
                    need(dve, p_norm, t)
                    dve.reciprocal(rinv[:, :], rsum[:, :]).then_inc(s_inv, 1)
                if ffn:
                    dve.wait_ge(f_ps, t - 1)
                    dve.wait_ge(x1b_sb, t - 1)
                    need(dve, stored, 16 * (t - 2))
                    dve.tensor_tensor(ost[:, :], bank(2), x1b[:, j % 2, :], ALU.add).then_inc(f_out, 1)

            dve.memset(ones[:, :], 1.0)
            lg, mx, e8, att = small[:, 16:24], small[:, 40:48], small[:, 32:40], small[:, 24:32]
            dve.wait_ge(su_pe, 3)
            dve.tensor_tensor(lg, bank(2)[:, 0:NE], small[:, 8:16], ALU.add).then_inc(su_dve, 1)
            dve.wait_ge(su_dve, 1)
            dve.max(mx, lg).then_inc(su_dve, 1)
            dve.wait_ge(su_dve, 2)
            dve.tensor_scalar(lg, lg, mx[:, 0:1], None, ALU.subtract).then_inc(su_dve, 1)
            dve.wait_ge(su_act, 3)
            dve.tensor_reduce(small[:, 48:49], e8, AX.X, ALU.add).then_inc(su_dve, 1)
            dve.wait_ge(su_dve, 4)
            dve.reciprocal(small[:, 49:50], small[:, 48:49]).then_inc(su_dve, 1)
            dve.wait_ge(su_dve, 5)
            dve.tensor_scalar(att, e8, small[:, 49:50], None, ALU.mult).then_inc(su_dve, 1)
            dve.wait_ge(su_pe, 5)
            dve.tensor_copy(attT, bank(3)[0:NE, 0:P]).then_inc(su_dve, 1)
            dve.wait_ge(su_pe, 6)
            dve.tensor_copy(aggb[:, :], bank(2)[:, 16:16 + T]).then_inc(su_dve, 1)
            dve.wait_ge(su_dve, 8)
            dve.wait_ge(ld_const, 16)
            lay_bias(0)
            dve.tensor_scalar(cbias[:, :], bank(6)[:, 0:NT], fside, None, ALU.add).then_inc(su_dve, 1)
            dve.tensor_copy(identb[:, :], ident).then_inc(su_dve, 1)
            dve.tensor_copy(maskb[:, :], const[:, C_MASK:C_MASK + C]).then_inc(su_dve, 1)
            keep_bias(0)

            def low(n):
                dve.wait_ge(whi_done[n], 1)
                dve.tensor_tensor(w_lo[n][:, :, :], staged[n], w_hi[n][:, :, :].bitcast(F32),
                                  ALU.subtract).then_inc(wlo_done[n], 1)
            low("wq")
            low("wk")
            y_full(0, 0, 0)
            low("wv")
            low("wo")
            low("wb")
            run_slots(dve, slot)

        @block.gpsimd
        def _(pool):
            def y_low(t):
                pool.wait_ge(y_hi, t + 1)
                need(pool, v_ps, t)
                pool.tensor_tensor(ylo[:, :, :], yf[:, :, :], yhi[:, :, :].bitcast(F32),
                                   ALU.subtract).then_inc(y_lo, 1)

            def slot(t, m, j, cur, prev, nxt, ffn):
                if ffn:
                    need(pool, z_sb, t - 2)
                    pool.tensor_copy(zbias[:, :], cbias[:, at(t - 2, 1)]).then_inc(zb_sb, 1)
                if cur:
                    pool.wait_ge(kT_sb, t + 1)
                    need(pool, s_ps, t)
                    pool.tensor_tensor(kbd[:, :, 3, :], kT[:, :, :],
                                       kmask[:, 3:4, None].to_broadcast([P, CK, P]), ALU.mult).then_inc(kbd_g, 1)
                if nxt:
                    y_low(t + 1)
                if ffn:
                    pool.wait_ge(z_hi, t - 1)
                    need(pool, f_ps, t - 2)
                    pool.tensor_tensor(zlo[:, :, :], zTf[:, :, :], zhi[:, :, :].bitcast(F32),
                                       ALU.subtract).then_inc(z_lo, 1)
                if prev:
                    pool.wait_ge(x1_sb, t)
                    need(pool, f_out, t - 2)
                    pool.tensor_tensor(x1b[:, (j - 1) % 2, :], x1[:, :], bbase[:, :],
                                       ALU.add).then_inc(x1b_sb, 1)
                if cur:
                    pool.wait_ge(s_inv, t + 1)
                    e3 = es[:, :].rearrange("p (h k) -> p h k", k=T)
                    pool.tensor_tensor(e3, e3, rinv[:, :, None].to_broadcast([P, H, T]),
                                       ALU.mult).then_inc(p_norm, 1)

            pool.memset(mixT[:, :, :], 0.0).then_inc(zeroed, 1)
            pool.memset(x3[:, :, :], 0.0).then_inc(zeroed, 1)
            pool.wait_ge(whi_done["wk"], 1)
            pool.wait_ge(wlo_done["wk"], 1)
            pool.memset(vbd[:, :, :, :], 0.0).then_inc(zeroed, 2)
            y_low(0)
            pool.wait_ge(ld_misc, 16 * 5)
            pool.wait_ge(su_dve, 11)
            for n in names:
                pool.wait_ge(wlo_done[n], 1)
            run_slots(pool, slot)


def launch(nc, shapes, out_shape):
    io = {n: nc.dram_tensor("in_" + n, s, F32, kind="ExternalInput").ap() for n, s in shapes.items()}
    io["out"] = nc.dram_tensor("out_0", out_shape, F32, kind="ExternalOutput").ap()
    build(nc, io)


def constants():
    c = np.zeros((P, NC), np.float32)
    p = np.arange(P)
    c[:, C_ID:C_ID + P] = np.eye(P)
    angle = (p % T).astype(np.float32)
    cos, sin, scale = np.cos(angle), np.sin(angle), np.float32(HD ** -0.5)
    for n, v in enumerate((cos * scale, sin * scale, -sin * scale, cos, sin, -sin)):
        c[:, C_ROT + n] = v
    for h in range(4):
        c[:, C_KM + h] = (p // HD) % 4 == h
    c[:, C_IO:C_IO + 8] = np.arange(8)
    k = np.arange(C) % T
    c[:, C_MASK:C_MASK + C] = np.where(k[None, :] <= (p % T)[:, None], 0.0, -1e30)
    return c


def kernel(x, cond_128, fside_S_0, L0_cond_W0, L0_cond_b0, L0_cond_W1, L0_cond_b1, L0_cond_W2, L0_cond_b2,
           L0_cond_weight, L0_cond_bias_k, L0_attn_wq, L0_attn_wk, L0_attn_wv, L0_attn_wo, L0_cond2_weight,
           L0_cond2_c_weight, L0_ffn_W_base, L0_ffn_b_base, L0_ffn_W_gate, L0_ffn_A, L0_ffn_B):
    import concourse.bacc as bacc
    from concourse.bass_utils import run_bass_kernel_spmd

    def chunked(w):
        return w.reshape(CK, P, -1).transpose(1, 0, 2)

    pair = np.arange(C).reshape(H, HD // 2, 2).transpose(0, 2, 1).reshape(-1)
    heads = np.arange(H).reshape(CK, 2, 4).transpose(1, 0, 2)
    v_cols = (heads.transpose(2, 0, 1)[..., None] * HD + np.arange(HD)).reshape(-1)
    o_rows = (heads[..., None] * HD + np.arange(HD)).reshape(-1)

    wc = np.asarray(L0_cond2_weight).reshape(T, 8, TAPS // SH, SH)
    conv = np.zeros((SH, T, TAPS // SH, T), np.float32)
    for g in range(4):
        own = slice(8 * g, 8 * g + 8)
        conv[:, own, :, own] = wc[own].transpose(3, 1, 2, 0)

    arrays = {
        "x": np.asarray(x).reshape(B * T, C),
        "condT": np.asarray(cond_128).T,
        "W0": L0_cond_W0, "b0": np.asarray(L0_cond_b0).reshape(P, 1),
        "W1": L0_cond_W1, "b1": np.asarray(L0_cond_b1).reshape(P, 1),
        "W2": L0_cond_W2, "b2": np.asarray(L0_cond_b2).reshape(1, NE),
        "cw": np.asarray(L0_cond_weight).reshape(NE, T * T),
        "biask": L0_cond_bias_k,
        "cwT": np.asarray(L0_cond2_c_weight).T,
        "fside": np.tile(np.asarray(fside_S_0), BPT).reshape(P, 1),
        "wq": chunked(np.asarray(L0_attn_wq).T[:, pair]),
        "wk": chunked(np.asarray(L0_attn_wk).T[:, pair]),
        "wv": chunked(np.asarray(L0_attn_wv).T[:, v_cols]),
        "wo": chunked(np.asarray(L0_attn_wo).T[o_rows]),
        "wb": chunked(np.asarray(L0_ffn_W_base).T),
        "wa": chunked(np.asarray(L0_ffn_A).reshape(NA, C).T),
        "wg": chunked(np.asarray(L0_ffn_W_gate).T),
        "wbt": np.asarray(L0_ffn_B).transpose(0, 2, 1).reshape(NA, C),
        "bbase": np.asarray(L0_ffn_b_base).reshape(1, C),
        "wconv": conv.reshape(SH * T, TAPS // SH, T),
        "const": constants(),
    }
    arrays = {n: np.ascontiguousarray(a) for n, a in arrays.items()}
    nc = bacc.Bacc("TRN2", target_bir_lowering=False, num_devices=1)
    launch(nc, {n: a.shape for n, a in arrays.items()}, (B * T, C))
    r = run_bass_kernel_spmd(nc, [{"in_" + n: a for n, a in arrays.items()}], core_ids=[0])
    return r.results[0]["out_0"].reshape(B, T, C)
```

```python
import numpy as np
import concourse.bass as bass
from concourse import mybir
from contextlib import ExitStack

F32 = mybir.dt.float32
F32R = mybir.dt.float32r
U32 = mybir.dt.uint32
ALU = mybir.AluOpType
ACT = mybir.ActivationFunctionType
AX = mybir.AxisListType

P = 128
B, T, C = 128, 32, 512
H, HD = 32, 16
BPT = P // T
NT = B // BPT
TPM = 4
NM = NT // TPM
CK = C // P
MCOL = TPM * P
NE, RANK = 8, 16
NA = NE * RANK
NG = NA + NE
TAPS, PAD = 9, 4
SH = 3
XW = C + 2 * PAD
BANK = 512

C_ID, C_ROT, C_KM, C_IO, C_MASK = 0, 128, 134, 138, 146
NC = C_MASK + T


def build(nc, io):
    ctx = ExitStack()
    with ctx:
        def sb(name, shape, dt=F32):
            return ctx.enter_context(nc.sbuf_tensor(name, shape, dt))

        def sem(name):
            return ctx.enter_context(nc.semaphore(name))

        names = ["wq", "wk", "wv", "wo", "wb"]
        w_hi = {n: sb(n + "_hi", [P, CK, C], F32R) for n in names}
        w_lo = {n: sb(n + "_lo", [P, CK, C], F32R) for n in names}
        const = sb("const", [P, NC])
        ones = sb("ones", [P, P])
        wag = sb("wag", [P, CK, NG])
        wbt = sb("wbt", [P, C])
        wconv = sb("wconv", [SH * T, TAPS // SH, T])
        bbase = sb("bbase", [P, C])
        mixT = sb("mixT", [P, NT, P])
        cbias = sb("cbias", [P, NT])
        xst = sb("xst", [P, CK, C])
        aggb = sb("aggb", [P, T])
        xin = sb("xin", [P, TPM, C])
        x1 = sb("x1", [P, C])
        x1b = sb("x1b", [P, 2, C])
        x3 = sb("x3", [SH * T, BPT, XW])
        aggbc = sb("aggbc", [P, MCOL])
        xdiag = sb("xdiag", [P, MCOL])
        yf = sb("yf", [P, CK, P])
        yhi = sb("yhi", [P, CK, P], F32R)
        ylo = sb("ylo", [P, CK, P], F32R)
        qr = sb("qr", [P, C])
        kr = sb("kr", [P, C])
        qT = sb("qT", [P, CK, P])
        kT = sb("kT", [P, CK, P])
        kbd = sb("kbd", [P, CK, 4, P])
        vsb = sb("vsb", [P, 4, P])
        vbd = sb("vbd", [P, BPT, 4, P])
        es = sb("es", [P, H * T])
        pT = sb("pT", [P, H // 4, P])
        onat = sb("onat", [P, C])
        ohi = sb("ohi", [P, CK, P], F32R)
        olo = sb("olo", [P, CK, P], F32R)
        zsb = sb("zsb", [P, C])
        zTf = sb("zTf", [P, CK, P])
        zhi = sb("zhi", [P, CK, P], F32R)
        zlo = sb("zlo", [P, CK, P], F32R)
        zbias = sb("zbias", [P, 1])
        ost = sb("ost", [P, C])
        hw = sb("hw", [P, NA])
        hwT = sb("hwT", [P, NA])
        rmx = sb("rmx", [P, H])
        rsum = sb("rsum", [P, H])
        rinv = sb("rinv", [P, H])
        r8 = sb("r8", [P, 72])
        ri = sb("ri", [P, 8], U32)

        ps = ctx.enter_context(nc.psum_tensor("ps", [P, 8 * BANK], F32))

        def bank(n, width=1):
            return ps[:, n * BANK:(n + width) * BANK]

        condT = kr[:, 0:B]
        W0, W1 = es[:, 0:128], es[:, 128:256]
        h1, h2 = es[:, 256:384], es[:, 384:512]
        W2 = es[:, 512:520]
        small = es[:, 520:600]
        cwsb = pT[:, :, :].rearrange("p a b -> p (a b)")[0:8, 0:T * T]
        attT = qr[0:8, 0:B]
        biask = qr[0:8, 128:160]
        cwT = kr[:, 128:128 + T]
        fside = kr[:, 160:161]
        stage = [xst[:, :, :]] + [t[:, :, :, :].rearrange("p a b c -> p a (b c)") for t in (vbd, kbd)]
        staged = {"wq": stage[0], "wk": stage[1], "wv": stage[2], "wo": stage[0], "wb": stage[0]}

        ident = const[:, C_ID:C_ID + P]
        rot = const[:, C_ROT:C_ROT + 6]
        kmask = const[:, C_KM:C_KM + 4]
        iota8 = const[:, C_IO:C_IO + 8]
        mask = const[:, C_MASK:C_MASK + T]

        ld_first = sem("ld_first")
        ld_cond, ld_const, ld_misc = sem("ld_cond"), sem("ld_const"), sem("ld_misc")
        ld_w = {n: sem("ld_" + n) for n in names}
        ld_x = [sem(f"ld_x{j}") for j in range(TPM)]
        whi_done = {n: sem(f"whi_{n}") for n in names}
        wlo_done = {n: sem(f"wlo_{n}") for n in names}
        mix_ps, mix_a, mix_v = sem("mix_ps"), sem("mix_a"), sem("mix_v")
        zeroed, su_pe, su_act, su_dve = sem("zeroed"), sem("su_pe"), sem("su_act"), sem("su_dve")
        bc_d, bc_ps, bc_sb = sem("bc_d"), sem("bc_ps"), sem("bc_sb")
        cond_ps, y_f, y_hi, y_lo = sem("cond_ps"), sem("y_f"), sem("y_hi"), sem("y_lo")
        q_ps, k_ps, v_ps = sem("q_ps"), sem("k_ps"), sem("v_ps")
        q_cos, k_cos, v_sb, v_bd = sem("q_cos"), sem("k_cos"), sem("v_sb"), sem("v_bd")
        q_rot, k_rot = sem("q_rot"), sem("k_rot")
        tq_ps, tk_ps, qT_sb, kT_sb = sem("tq_ps"), sem("tk_ps"), sem("qT_sb"), sem("kT_sb")
        kbd_v, kbd_g = sem("kbd_v"), sem("kbd_g")
        s_mask = sem("s_mask")
        s_ps, s_max, s_sub, s_exp, s_sum, s_inv, p_norm = (
            sem("s_ps"), sem("s_max"), sem("s_sub"), sem("s_exp"), sem("s_sum"), sem("s_inv"), sem("p_norm"))
        pt_ps, pT_a, pT_v, pv_ps, o_sb = sem("pt_ps"), sem("pT_a"), sem("pT_v"), sem("pv_ps"), sem("o_sb")
        to_ps, o_hi, o_lo, wo_ps = sem("to_ps"), sem("o_hi"), sem("o_lo"), sem("wo_ps")
        x1_sb, x1b_sb, x3_sb = sem("x1_sb"), sem("x1b_sb"), sem("x3_sb")
        conv_ps, zb_sb, z_sb = sem("conv_ps"), sem("zb_sb"), sem("z_sb")
        tz_ps, z_f, z_hi, z_lo = sem("tz_ps"), sem("z_f"), sem("z_hi"), sem("z_lo")
        ag_ps, r_top, r_sub, r_exp, r_step, hw_sb = (
            sem("ag_ps"), sem("r_top"), sem("r_sub"), sem("r_exp"), sem("r_step"), sem("hw_sb"))
        ht_ps, hwT_sb, f_ps, f_out, stored = (
            sem("ht_ps"), sem("hwT_sb"), sem("f_ps"), sem("f_out"), sem("stored"))

        def need(eng, s, value):
            if isinstance(value, int) and value <= 0:
                return
            eng.wait_ge(s, value)

        def at(t, n=P):
            return slice(t * n, t * n + n) if isinstance(t, int) else bass.ds(t * n, n)

        def rows(eng, t):
            return at(t) if isinstance(t, int) else bass.ds(eng.snap(t * P), P)

        def run_slots(eng, slot):
            def four(m, first=False, last=False):
                for j in range(TPM):
                    slot(TPM * m + j, m, j, cur=True, prev=not (first and j == 0),
                         nxt=not (last and j == TPM - 1), ffn=not (first and j < 2),
                         end=not (first and j < 3))
            four(0, first=True)
            with eng.Fori(1, NM - 1) as m:
                four(m)
            four(NM - 1, last=True)
            slot(NT, NM, 0, cur=False, prev=True, nxt=False, ffn=True, end=True)
            slot(NT + 1, NM, 1, cur=False, prev=False, nxt=False, ffn=True, end=True)
            slot(NT + 2, NM, 2, cur=False, prev=False, nxt=False, ffn=False, end=True)

        def is_slot(t, n):
            return isinstance(t, int) and t == n

        def keep_mixing(eng, copy, half, batches, done):
            eng.wait_ge(mix_ps, half + 1)
            eng.wait_ge(zeroed, 1)
            for r in batches:
                own = slice(32 * r, 32 * r + 32)
                ins = copy(mixT[own, :, 32 * r + 16 * half:32 * r + 16 * half + 16],
                           bank(4 + half)[own, :].rearrange("i (o s) -> i s o", s=NT))
            ins.then_inc(done, 1)

        block = ctx.enter_context(nc.Block())

        @block.sync
        def _(sp):
            for dst, name in ((condT, "condT"), (W0, "W0"), (small[:, 0:1], "b0")):
                sp.dma_start(dst, io[name]).then_inc(ld_first, 16)
            for dst, name in ((W1, "W1"), (small[:, 1:2], "b1"), (W2, "W2")):
                sp.dma_start(dst, io[name]).then_inc(ld_cond, 16)
            sp.dma_start(small[:, 8:16], io["b2"].to_broadcast([P, NE])).then_inc(ld_cond, 16)
            sp.dma_start(cwsb, io["cw"]).then_inc(ld_cond, 16)
            sp.dma_start(biask, io["biask"]).then_inc(ld_cond, 16)
            sp.dma_start(cwT, io["cwT"]).then_inc(ld_cond, 16)
            sp.dma_start(fside, io["fside"]).then_inc(ld_cond, 16)
            sp.dma_start(xin[:, 0, :], io["x"][0:P, :]).then_inc(ld_x[0], 16)
            for n in ("wq", "wk", "wv"):
                sp.dma_start(staged[n], io[n]).then_inc(ld_w[n], 16)
            for j in range(1, TPM):
                sp.dma_start(xin[:, j, :], io["x"][at(j), :]).then_inc(ld_x[j], 16)
            sp.dma_start(wconv[:, :, :], io["wconv"]).then_inc(ld_misc, 16)
            sp.dma_start(wag[:, :, 0:NA], io["wa"]).then_inc(ld_misc, 16)
            sp.dma_start(wag[:, :, NA:NG], io["wg"]).then_inc(ld_misc, 16)
            sp.dma_start(wbt[:, :], io["wbt"]).then_inc(ld_misc, 16)
            sp.dma_start(bbase[:, :], io["bbase"].to_broadcast([P, C])).then_inc(ld_misc, 16)

            def load_late(n, before):
                sp.wait_ge(whi_done[before], 1)
                sp.wait_ge(wlo_done[before], 1)
                sp.dma_start(staged[n], io[n]).then_inc(ld_w[n], 16)

            load_late("wo", "wq")

            def slot(t, m, j, cur, prev, nxt, ffn, end):
                more = prev and not (isinstance(t, int) and t + TPM - 1 >= NT)
                x_rows = rows(sp, t + TPM - 1) if more else None
                out_rows = rows(sp, t - 3) if end else None
                if end:
                    sp.wait_ge(f_out, t - 2)
                    sp.dma_start(io["out"][out_rows, :], ost[:, :]).then_inc(stored, 16)
                if cur:
                    sp.wait_ge(v_sb, t + 1)
                    need(sp, pv_ps, t)
                    if isinstance(t, int) and t == 0:
                        sp.wait_ge(zeroed, 4)
                    for h in range(4):
                        for b in range(BPT):
                            sp.dma_start(vbd[32 * h:32 * h + 32, b, h, :],
                                         vsb[32 * b:32 * b + 32, h, :]).then_inc(v_bd, 16)
                if is_slot(t, 0):
                    load_late("wb", "wo")
                if prev:
                    sp.wait_ge(x1_sb, t)
                    for s_ in range(SH):
                        for b in range(BPT):
                            sp.dma_start(x3[32 * s_:32 * s_ + 32, b, PAD - s_:PAD - s_ + C],
                                         x1[32 * b:32 * b + 32, :]).then_inc(x3_sb, 16)
                    if more:
                        jn = (j - 1) % TPM
                        sp.dma_start(xin[:, jn, :], io["x"][x_rows, :]).then_inc(ld_x[jn], 16)

            run_slots(sp, slot)
            sp.wait_ge(stored, 16 * NT)

        @block.tensor
        def _(pe):
            def split_mm(out, hi, lo, name, last=True):
                parts = ((hi, w_hi[name]), (hi, w_lo[name]), (lo, w_hi[name]))
                for a, (x, w) in enumerate(parts):
                    for c in range(CK):
                        mm = pe.matmul(out, x[:, c, :], w[:, c, :], start=(a == 0 and c == 0),
                                       stop=(last and a == 2 and c == CK - 1), skip_group_check=True)
                return mm

            def turn(n, src, done):
                for c in range(CK):
                    mm = pe.transpose(bank(n)[:, c * P:(c + 1) * P], src[:, c * P:(c + 1) * P], ident)
                mm.then_inc(done, 1)

            def broadcast_bias(m, first=False):
                pe.wait_ge(bc_d, m + 1)
                if not first:
                    pe.wait_ge(x1_sb, TPM * m - 2)
                pe.matmul(bank(7), ones[:, :], xdiag[:, :], start=True, stop=True).then_inc(bc_ps, 1)

            def mix(t, m, j):
                pe.wait_ge(ld_x[j], 16 * (m + 1))
                mixing = mixT[:, t, :] if isinstance(t, int) else \
                    mixT[:, bass.ds(t, 1), :].rearrange("p o c -> p (o c)")
                for c in range(CK):
                    mm = pe.matmul(bank(7)[:, c * P:(c + 1) * P], xin[:, j, c * P:(c + 1) * P], mixing,
                                   start=True, stop=True, skip_group_check=True)
                mm.then_inc(cond_ps, 1)

            def weights(name):
                pe.wait_ge(whi_done[name], 1)
                pe.wait_ge(wlo_done[name], 1)

            def slot(t, m, j, cur, prev, nxt, ffn, end):
                if cur:
                    if is_slot(t, 0):
                        weights("wq")
                    pe.wait_ge(y_hi, t + 1)
                    pe.wait_ge(y_lo, t + 1)
                    need(pe, o_lo, t - 1)
                    split_mm(bank(6), yhi, ylo, "wq").then_inc(q_ps, 1)
                if end:
                    pe.wait_ge(hw_sb, t - 2)
                    pe.transpose(bank(5)[:, 256:256 + NA], hw[:, :], ident).then_inc(ht_ps, 1)
                if cur:
                    if is_slot(t, 0):
                        weights("wk")
                    need(pe, o_sb, t - 1)
                    split_mm(bank(4), yhi, ylo, "wk").then_inc(k_ps, 1)
                if end:
                    pe.wait_ge(hwT_sb, t - 2)
                    pe.matmul(bank(2), hwT[:, :], wbt[:, :], start=False, stop=True,
                              skip_group_check=True).then_inc(f_ps, 1)
                if cur:
                    if is_slot(t, 0):
                        weights("wv")
                    split_mm(bank(5), yhi, ylo, "wv").then_inc(v_ps, 1)
                if nxt and j == TPM - 1:
                    broadcast_bias(m + 1)
                if cur:
                    pe.wait_ge(q_rot, t + 1)
                    need(pe, f_out, t - 2)
                    turn(2, qr, tq_ps)
                    pe.wait_ge(k_rot, t + 1)
                    turn(3, kr, tk_ps)
                if prev:
                    pe.wait_ge(p_norm, t)
                    for g in range(H // 4):
                        mm = pe.transpose(bank(0, 2)[:, g * P:(g + 1) * P], es[:, g * P:(g + 1) * P], ident)
                    mm.then_inc(pt_ps, 1)
                if ffn:
                    if is_slot(t, 2):
                        pe.wait_ge(ld_misc, 16 * 5)
                    pe.wait_ge(x3_sb, 16 * SH * BPT * (t - 1))
                    if cur:
                        pe.wait_ge(q_rot, t + 1)
                    for g in range(TAPS // SH):
                        for b in range(BPT):
                            mm = pe.matmul(bank(6)[32 * b:32 * b + 32, :], wconv[:, g, :],
                                           x3[:, b, SH * g:SH * g + C], start=(g == 0),
                                           stop=(g == TAPS // SH - 1), skip_group_check=True)
                    mm.then_inc(conv_ps, 1)
                if prev:
                    pe.wait_ge(pT_a, t)
                    pe.wait_ge(pT_v, t)
                    pe.wait_ge(v_bd, 16 * 4 * BPT * t)
                    if cur:
                        pe.wait_ge(k_rot, t + 1)
                    for g in range(H // 4):
                        for b in range(BPT):
                            mm = pe.matmul(bank(4)[32 * b:32 * b + 32, g * 64:(g + 1) * 64],
                                           pT[:, g, 32 * b:32 * b + 32], vbd[:, b, :, g * HD:(g + 1) * HD],
                                           start=True, stop=True, skip_group_check=True)
                    mm.then_inc(pv_ps, 1)
                if ffn:
                    pe.wait_ge(z_sb, t - 1)
                    if cur:
                        pe.wait_ge(v_sb, t + 1)
                    turn(5, zsb, tz_ps)
                if nxt:
                    need(pe, x1_sb, t - 1)
                    if j == TPM - 1:
                        pe.wait_ge(bc_sb, m + 2)
                    mix(t + 1, m + (j + 1) // TPM, (j + 1) % TPM)
                if prev:
                    pe.wait_ge(o_sb, t)
                    need(pe, z_sb, t - 1)
                    turn(6, onat, to_ps)
                if ffn:
                    pe.wait_ge(z_f, t - 1)
                    for c in range(CK):
                        mm = pe.matmul(bank(5)[:, 0:NG], zTf[:, c, :], wag[:, c, :],
                                       start=(c == 0), stop=(c == CK - 1), skip_group_check=True)
                    mm.then_inc(ag_ps, 1)
                if cur:
                    pe.wait_ge(su_pe, 6)
                    pe.wait_ge(qT_sb, t + 1)
                    pe.wait_ge(kbd_v, t + 1)
                    pe.wait_ge(kbd_g, t + 1)
                    if prev:
                        pe.wait_ge(pT_a, t)
                        pe.wait_ge(pT_v, t)
                    for c in range(CK):
                        for g in range(2):
                            for b in range(BPT):
                                mm = pe.matmul(
                                    bank(g)[32 * b:32 * b + 32, c * P:(c + 1) * P],
                                    qT[64 * g:64 * g + 64, c, 32 * b:32 * b + 32],
                                    kbd[64 * g:64 * g + 64, c, :, 32 * b:32 * b + 32],
                                    start=True, stop=True, skip_group_check=True)
                    mm.then_inc(s_ps, 1)
                if prev:
                    if is_slot(t, 1):
                        weights("wo")
                    pe.wait_ge(o_hi, t)
                    pe.wait_ge(o_lo, t)
                    if nxt:
                        pe.wait_ge(y_f, t + 2)
                    split_mm(bank(7), ohi, olo, "wo").then_inc(wo_ps, 1)
                if ffn:
                    if is_slot(t, 2):
                        weights("wb")
                    pe.wait_ge(z_hi, t - 1)
                    pe.wait_ge(z_lo, t - 1)
                    if cur:
                        pe.wait_ge(qT_sb, t + 1)
                    else:
                        pe.wait_ge(f_out, t - 2)
                    split_mm(bank(2), zhi, zlo, "wb", last=False)

            pe.wait_ge(ld_first, 16 * 3)
            pe.matmul(bank(0)[:, 0:P], W0, condT, start=True, stop=True).then_inc(su_pe, 1)
            pe.wait_ge(ld_cond, 16 * 8)
            pe.wait_ge(su_act, 1)
            pe.matmul(bank(1)[:, 0:P], W1, h1, start=True, stop=True).then_inc(su_pe, 1)
            pe.wait_ge(su_act, 2)
            pe.matmul(bank(2)[:, 0:NE], h2, W2, start=True, stop=True).then_inc(su_pe, 1)
            condv = condT.rearrange("d (s r) -> d r s", r=BPT)
            for r in range(BPT):
                mm = pe.matmul(bank(6)[32 * r:32 * r + 32, 0:NT], cwT, condv[:, r, :],
                               start=True, stop=True, skip_group_check=True)
            mm.then_inc(su_pe, 1)
            pe.wait_ge(su_dve, 6)
            pe.wait_ge(ld_const, 16)
            pe.transpose(bank(3)[0:NE, 0:P], small[:, 24:32], ident).then_inc(su_pe, 1)
            pe.wait_ge(su_dve, 7)
            pe.matmul(bank(2)[:, 16:16 + T], attT, biask, start=True, stop=True).then_inc(su_pe, 1)
            cwv = cwsb.rearrange("k (o i) -> k o i", i=T)
            attv = attT.rearrange("k (s r) -> k r s", r=BPT)
            for half in range(2):
                for o in range(T // 2 * half, T // 2 * (half + 1)):
                    for r in range(BPT):
                        mm = pe.matmul(bank(4, 2)[32 * r:32 * r + 32, o * NT:(o + 1) * NT], cwv[:, o, :],
                                       attv[:, r, :], start=True, stop=True, skip_group_check=True)
                mm.then_inc(mix_ps, 1)
                if half == 0:
                    broadcast_bias(0, first=True)
            pe.wait_ge(bc_sb, 1)
            pe.wait_ge(mix_a, 2)
            pe.wait_ge(mix_v, 2)
            mix(0, 0, 0)
            run_slots(pe, slot)

        @block.scalar
        def _(act):
            def y_high(t):
                act.wait_ge(y_f, t + 1)
                need(act, v_ps, t)
                act.copy(yhi[:, :, :], yf[:, :, :]).then_inc(y_hi, 1)

            def four(n):
                return bank(n).rearrange("p (c r) -> p c r", c=CK)

            def high(n):
                act.wait_ge(ld_w[n], 16)
                act.copy(w_hi[n][:, :, :], staged[n]).then_inc(whi_done[n], 1)

            def slot(t, m, j, cur, prev, nxt, ffn, end):
                if cur:
                    act.wait_ge(q_ps, t + 1)
                    need(act, tq_ps, t)
                    act.activation(qr[:, :], bank(6), ACT.Copy, scale=rot[:, 0:1]).then_inc(q_cos, 1)
                if end:
                    act.wait_ge(ht_ps, t - 2)
                    need(act, f_ps, t - 3)
                    act.copy(hwT[:, :], bank(5)[:, 256:256 + NA]).then_inc(hwT_sb, 1)
                if cur:
                    act.wait_ge(k_ps, t + 1)
                    need(act, tk_ps, t)
                    act.activation(kr[:, :], bank(4), ACT.Copy, scale=rot[:, 3:4]).then_inc(k_cos, 1)
                    act.wait_ge(v_ps, t + 1)
                    need(act, v_bd, 16 * 4 * BPT * t)
                    act.copy(vsb[:, :, :], four(5)).then_inc(v_sb, 1)
                    act.wait_ge(tq_ps, t + 1)
                    need(act, s_ps, t)
                    act.copy(qT[:, :, :], four(2)).then_inc(qT_sb, 1)
                    act.wait_ge(tk_ps, t + 1)
                    need(act, kbd_v, t)
                    need(act, kbd_g, t)
                    act.copy(kT[:, :, :], four(3)).then_inc(kT_sb, 1)
                if prev:
                    act.wait_ge(pt_ps, t)
                    need(act, pv_ps, t - 1)
                    act.copy(pT[:, 0:4, :], four(0)).then_inc(pT_a, 1)
                if ffn:
                    act.wait_ge(conv_ps, t - 1)
                    act.wait_ge(zb_sb, t - 1)
                    need(act, tz_ps, t - 2)
                    act.activation(zsb[:, :], bank(6), ACT.Identity, bias=zbias[:, 0:1]).then_inc(z_sb, 1)
                if prev:
                    act.wait_ge(pv_ps, t)
                    need(act, to_ps, t - 1)
                    act.copy(onat[:, :], bank(4)).then_inc(o_sb, 1)
                if ffn:
                    act.wait_ge(tz_ps, t - 1)
                    need(act, ag_ps, t - 2)
                    need(act, z_lo, t - 2)
                    act.copy(zTf[:, :, :], four(5)).then_inc(z_f, 1)
                if nxt:
                    y_high(t + 1)
                if prev:
                    act.wait_ge(to_ps, t)
                    need(act, wo_ps, t - 1)
                    act.copy(ohi[:, :, :], four(6)).then_inc(o_hi, 1)
                if ffn:
                    act.wait_ge(r_sub, t - 1)
                    act.activation(r8[:, 16:24], r8[:, 8:16], ACT.Exp).then_inc(r_exp, 1)
                if cur:
                    act.wait_ge(s_sub, t + 1)
                    act.activation(es[:, :], es[:, :], ACT.Exp).then_inc(s_exp, 1)
                if is_slot(t, 0):
                    high("wo")
                if is_slot(t, 1):
                    high("wb")

            act.dma_start(const[:, :], io["const"]).then_inc(ld_const, 16)
            act.wait_ge(ld_first, 16 * 3)
            act.wait_ge(su_pe, 1)
            act.activation(h1, bank(0)[:, 0:P], ACT.Gelu, bias=small[:, 0:1]).then_inc(su_act, 1)
            act.wait_ge(ld_cond, 16 * 8)
            act.wait_ge(su_pe, 2)
            act.activation(h2, bank(1)[:, 0:P], ACT.Gelu, bias=small[:, 1:2]).then_inc(su_act, 1)
            act.wait_ge(su_dve, 3)
            act.activation(small[:, 32:40], small[:, 16:24], ACT.Exp).then_inc(su_act, 1)
            high("wq")
            high("wk")
            for half in range(2):
                keep_mixing(act, act.copy, half, (0, 1), mix_a)
            y_high(0)
            high("wv")
            run_slots(act, slot)

        @block.vector
        def _(dve):
            def four(n):
                return bank(n).rearrange("p (c r) -> p c r", c=CK)

            def rotate(dst, src, k, done):
                d = dst[:, :].rearrange("p (h two e) -> p h two e", two=2, e=HD // 2)
                s = src.rearrange("p (h two e) -> p h two e", two=2, e=HD // 2)
                dve.scalar_tensor_tensor(out=d[:, :, 0, :], in0=s[:, :, 1, :], scalar=rot[:, k + 2:k + 3],
                                         in1=d[:, :, 0, :], op0=ALU.mult, op1=ALU.add)
                dve.scalar_tensor_tensor(out=d[:, :, 1, :], in0=s[:, :, 0, :], scalar=rot[:, k + 1:k + 2],
                                         in1=d[:, :, 1, :], op0=ALU.mult, op1=ALU.add).then_inc(done, 1)

            def lay_bias(m):
                need(dve, bc_ps, m)
                own = (const[:, C_ID + 16 * m:C_ID + 16 * m + 16] if isinstance(m, int) else
                       const[:, bass.ds(C_ID + 16 * m, 16)])
                dve.tensor_tensor(xdiag[:, :].rearrange("p (b t) -> p b t", t=T),
                                  aggb[:, None, :].to_broadcast([P, 16, T]),
                                  own[:, :, None].to_broadcast([P, 16, T]), ALU.mult).then_inc(bc_d, 1)

            def keep_bias(m):
                dve.wait_ge(bc_ps, m + 1)
                dve.tensor_copy(aggbc[:, :], bank(7)).then_inc(bc_sb, 1)

            def y_full(t, m, j):
                dve.wait_ge(cond_ps, t + 1)
                need(dve, y_hi, t)
                need(dve, y_lo, t)
                if j == 0:
                    dve.wait_ge(bc_sb, m + 1)
                dve.tensor_tensor(yf[:, :, :], four(7),
                                  aggbc[:, None, j * P:(j + 1) * P].to_broadcast([P, CK, P]),
                                  ALU.add).then_inc(y_f, 1)

            def route(t):
                f = t - 2
                dve.wait_ge(ag_ps, f + 1)
                dve.tensor_reduce(r8[:, 0:1], bank(5)[:, NA:NG], AX.X, ALU.max).then_inc(r_top, 1)
                dve.wait_ge(r_top, 2 * f + 1)
                need(dve, r_exp, f)
                dve.tensor_scalar(r8[:, 8:16], bank(5)[:, NA:NG], r8[:, 0:1], None,
                                  ALU.subtract).then_inc(r_sub, 1)

            def route_rest(t):
                f = t - 2
                dve.wait_ge(su_dve, 9)
                dve.wait_ge(r_exp, f + 1)
                dve.max(r8[:, 24:32], r8[:, 16:24]).then_inc(r_top, 1)
                dve.wait_ge(r_top, 2 * f + 2)
                dve.tensor_tensor(r8[:, 64:65], r8[:, 24:25], r8[:, 25:26], ALU.add).then_inc(r_step, 1)
                dve.max_index(ri[:, :], r8[:, 24:32], r8[:, 16:24]).then_inc(r_step, 1)
                dve.wait_ge(r_step, 6 * f + 2)
                dve.tensor_copy(r8[:, 32:40], ri[:, :]).then_inc(r_step, 1)
                dve.reciprocal(r8[:, 65:66], r8[:, 64:65])
                dve.wait_ge(r_step, 6 * f + 3)
                dve.tensor_scalar(r8[:, 40:48], iota8, r8[:, 32:33], r8[:, 24:25], ALU.is_equal,
                                  ALU.mult).then_inc(r_step, 1)
                dve.tensor_scalar(r8[:, 48:56], iota8, r8[:, 33:34], r8[:, 25:26], ALU.is_equal,
                                  ALU.mult).then_inc(r_step, 1)
                dve.wait_ge(r_step, 6 * f + 5)
                dve.tensor_tensor(r8[:, 56:64], r8[:, 40:48], r8[:, 48:56], ALU.add).then_inc(r_step, 1)
                dve.wait_ge(r_step, 6 * f + 6)
                need(dve, ht_ps, f)
                dve.scalar_tensor_tensor(out=hw[:, :].rearrange("p (e r) -> p e r", e=NE),
                                         in0=bank(5)[:, 0:NA].rearrange("p (e r) -> p e r", e=NE),
                                         scalar=r8[:, 65:66],
                                         in1=r8[:, 56:64, None].to_broadcast([P, NE, RANK]),
                                         op0=ALU.mult, op1=ALU.mult).then_inc(hw_sb, 1)

            def low(n):
                dve.wait_ge(whi_done[n], 1)
                dve.tensor_tensor(w_lo[n][:, :, :], staged[n], w_hi[n][:, :, :].bitcast(F32),
                                  ALU.subtract).then_inc(wlo_done[n], 1)

            def slot(t, m, j, cur, prev, nxt, ffn, end):
                if cur:
                    dve.wait_ge(q_cos, t + 1)
                    rotate(qr, bank(6), 0, q_rot)
                    dve.wait_ge(k_cos, t + 1)
                    rotate(kr, bank(4), 3, k_rot)
                if end:
                    dve.wait_ge(f_ps, t - 2)
                    dve.wait_ge(x1b_sb, t - 2)
                    need(dve, stored, 16 * (t - 3))
                    dve.tensor_tensor(ost[:, :], bank(2), x1b[:, (j - 3) % 2, :], ALU.add).then_inc(f_out, 1)
                if nxt and j == TPM - 1:
                    lay_bias(m + 1)
                    keep_bias(m + 1)
                if cur:
                    dve.wait_ge(kT_sb, t + 1)
                    need(dve, s_ps, t)
                    if is_slot(t, 0):
                        dve.wait_ge(wlo_done["wv"], 1)
                    for h in range(3):
                        ins = dve.tensor_scalar(kbd[:, :, h, :], kT[:, :, :], kmask[:, h:h + 1], None, ALU.mult)
                    ins.then_inc(kbd_v, 1)
                if prev:
                    dve.wait_ge(pt_ps, t)
                    need(dve, pv_ps, t - 1)
                    dve.tensor_copy(pT[:, 4:8, :], four(1)).then_inc(pT_v, 1)
                if nxt:
                    y_full(t + 1, m + (j + 1) // TPM, (j + 1) % TPM)
                if ffn:
                    dve.wait_ge(z_f, t - 1)
                    need(dve, f_ps, t - 2)
                    dve.tensor_copy(zhi[:, :, :], zTf[:, :, :]).then_inc(z_hi, 1)
                if prev:
                    dve.wait_ge(o_hi, t)
                    need(dve, wo_ps, t - 1)
                    dve.tensor_tensor(olo[:, :, :], four(6), ohi[:, :, :].bitcast(F32),
                                      ALU.subtract).then_inc(o_lo, 1)
                if ffn:
                    route(t)
                    route_rest(t)
                if cur:
                    s3 = bank(0, 2).rearrange("p (h k) -> p h k", k=T)
                    e3 = es[:, :].rearrange("p (h k) -> p h k", k=T)
                    dve.wait_ge(s_ps, t + 1)
                    need(dve, pt_ps, t)
                    dve.tensor_tensor(e3, s3, mask[:, None, :].to_broadcast([P, H, T]),
                                      ALU.add).then_inc(s_mask, 1)
                    dve.wait_ge(s_mask, t + 1)
                    dve.tensor_reduce(rmx[:, :], e3, AX.X, ALU.max).then_inc(s_max, 1)
                    dve.wait_ge(s_max, t + 1)
                    dve.tensor_tensor(e3, e3, rmx[:, :, None].to_broadcast([P, H, T]),
                                      ALU.subtract).then_inc(s_sub, 1)
                if prev:
                    dve.wait_ge(wo_ps, t)
                    need(dve, x3_sb, 16 * SH * BPT * (t - 1))
                    need(dve, x1b_sb, t - 1)
                    dve.tensor_tensor(x1[:, :], bank(7), xin[:, (j - 1) % TPM, :],
                                      ALU.add).then_inc(x1_sb, 1)
                if cur:
                    dve.wait_ge(s_exp, t + 1)
                    dve.tensor_reduce(rsum[:, :], e3, AX.X, ALU.add).then_inc(s_sum, 1)
                    dve.wait_ge(s_sum, t + 1)
                    need(dve, p_norm, t)
                    dve.reciprocal(rinv[:, :], rsum[:, :]).then_inc(s_inv, 1)
                if is_slot(t, 0):
                    low("wo")
                if is_slot(t, 1):
                    low("wb")

            dve.memset(ones[:, :], 1.0)
            lg, mx, e8, att = small[:, 16:24], small[:, 40:48], small[:, 32:40], small[:, 24:32]
            dve.wait_ge(su_pe, 3)
            dve.tensor_tensor(lg, bank(2)[:, 0:NE], small[:, 8:16], ALU.add).then_inc(su_dve, 1)
            dve.wait_ge(su_dve, 1)
            dve.max(mx, lg).then_inc(su_dve, 1)
            dve.wait_ge(su_dve, 2)
            dve.tensor_scalar(lg, lg, mx[:, 0:1], None, ALU.subtract).then_inc(su_dve, 1)
            dve.wait_ge(su_act, 3)
            dve.tensor_reduce(small[:, 48:49], e8, AX.X, ALU.add).then_inc(su_dve, 1)
            dve.wait_ge(su_dve, 4)
            dve.reciprocal(small[:, 49:50], small[:, 48:49]).then_inc(su_dve, 1)
            dve.wait_ge(su_dve, 5)
            dve.tensor_scalar(att, e8, small[:, 49:50], None, ALU.mult).then_inc(su_dve, 1)
            dve.wait_ge(su_pe, 5)
            dve.tensor_copy(attT, bank(3)[0:NE, 0:P]).then_inc(su_dve, 1)
            dve.wait_ge(su_pe, 6)
            dve.tensor_copy(aggb[:, :], bank(2)[:, 16:16 + T]).then_inc(su_dve, 1)
            dve.wait_ge(su_dve, 8)
            dve.wait_ge(ld_const, 16)
            lay_bias(0)
            dve.tensor_scalar(cbias[:, :], bank(6)[:, 0:NT], fside, None, ALU.add).then_inc(su_dve, 1)
            low("wq")
            keep_mixing(dve, dve.tensor_copy, 0, (2, 3), mix_v)
            keep_bias(0)
            low("wk")
            keep_mixing(dve, dve.tensor_copy, 1, (2, 3), mix_v)
            y_full(0, 0, 0)
            low("wv")
            run_slots(dve, slot)

        @block.gpsimd
        def _(pool):
            def y_low(t):
                pool.wait_ge(y_hi, t + 1)
                need(pool, v_ps, t)
                pool.tensor_tensor(ylo[:, :, :], yf[:, :, :], yhi[:, :, :].bitcast(F32),
                                   ALU.subtract).then_inc(y_lo, 1)

            def slot(t, m, j, cur, prev, nxt, ffn, end):
                if ffn:
                    need(pool, z_sb, t - 2)
                    pool.tensor_copy(zbias[:, :], cbias[:, at(t - 2, 1)]).then_inc(zb_sb, 1)
                if cur:
                    pool.wait_ge(kT_sb, t + 1)
                    need(pool, s_ps, t)
                    if is_slot(t, 0):
                        pool.wait_ge(wlo_done["wv"], 1)
                    pool.tensor_tensor(kbd[:, :, 3, :], kT[:, :, :],
                                       kmask[:, 3:4, None].to_broadcast([P, CK, P]), ALU.mult).then_inc(kbd_g, 1)
                if nxt:
                    y_low(t + 1)
                if ffn:
                    pool.wait_ge(z_hi, t - 1)
                    need(pool, f_ps, t - 2)
                    pool.tensor_tensor(zlo[:, :, :], zTf[:, :, :], zhi[:, :, :].bitcast(F32),
                                       ALU.subtract).then_inc(z_lo, 1)
                if prev:
                    if is_slot(t, 1):
                        pool.wait_ge(ld_misc, 16 * 5)
                    pool.wait_ge(x1_sb, t)
                    need(pool, f_out, t - 2)
                    pool.tensor_tensor(x1b[:, (j - 1) % 2, :], x1[:, :], bbase[:, :],
                                       ALU.add).then_inc(x1b_sb, 1)
                if cur:
                    pool.wait_ge(s_inv, t + 1)
                    e3 = es[:, :].rearrange("p (h k) -> p h k", k=T)
                    pool.tensor_tensor(e3, e3, rinv[:, :, None].to_broadcast([P, H, T]),
                                       ALU.mult).then_inc(p_norm, 1)

            pool.memset(mixT[:, :, :], 0.0).then_inc(zeroed, 1)
            pool.memset(x3[:, :, :], 0.0).then_inc(zeroed, 1)
            y_low(0)
            pool.wait_ge(whi_done["wk"], 1)
            pool.wait_ge(wlo_done["wk"], 1)
            pool.memset(vbd[:, :, :, :], 0.0).then_inc(zeroed, 2)
            pool.wait_ge(su_dve, 9)
            run_slots(pool, slot)


def launch(nc, shapes, out_shape):
    io = {n: nc.dram_tensor("in_" + n, s, F32, kind="ExternalInput").ap() for n, s in shapes.items()}
    io["out"] = nc.dram_tensor("out_0", out_shape, F32, kind="ExternalOutput").ap()
    build(nc, io)


def constants():
    c = np.zeros((P, NC), np.float32)
    p = np.arange(P)
    c[:, C_ID:C_ID + P] = np.eye(P)
    angle = (p % T).astype(np.float32)
    cos, sin, scale = np.cos(angle), np.sin(angle), np.float32(HD ** -0.5)
    for n, v in enumerate((cos * scale, sin * scale, -sin * scale, cos, sin, -sin)):
        c[:, C_ROT + n] = v
    for h in range(4):
        c[:, C_KM + h] = (p // HD) % 4 == h
    c[:, C_IO:C_IO + 8] = np.arange(8)
    c[:, C_MASK:C_MASK + T] = np.where(np.arange(T)[None, :] <= (p % T)[:, None], 0.0, -1e30)
    return c


def kernel(x, cond_128, fside_S_0, L0_cond_W0, L0_cond_b0, L0_cond_W1, L0_cond_b1, L0_cond_W2, L0_cond_b2,
           L0_cond_weight, L0_cond_bias_k, L0_attn_wq, L0_attn_wk, L0_attn_wv, L0_attn_wo, L0_cond2_weight,
           L0_cond2_c_weight, L0_ffn_W_base, L0_ffn_b_base, L0_ffn_W_gate, L0_ffn_A, L0_ffn_B):
    import concourse.bacc as bacc
    from concourse.bass_utils import run_bass_kernel_spmd

    def chunked(w):
        return w.reshape(CK, P, -1).transpose(1, 0, 2)

    pair = np.arange(C).reshape(H, HD // 2, 2).transpose(0, 2, 1).reshape(-1)
    heads = np.arange(H).reshape(CK, 2, 4).transpose(1, 0, 2)
    v_cols = (heads.transpose(2, 0, 1)[..., None] * HD + np.arange(HD)).reshape(-1)
    o_rows = (heads[..., None] * HD + np.arange(HD)).reshape(-1)

    wc = np.asarray(L0_cond2_weight).reshape(T, 8, TAPS // SH, SH)
    conv = np.zeros((SH, T, TAPS // SH, T), np.float32)
    for g in range(4):
        own = slice(8 * g, 8 * g + 8)
        conv[:, own, :, own] = wc[own].transpose(3, 1, 2, 0)

    arrays = {
        "x": np.asarray(x).reshape(B * T, C),
        "condT": np.asarray(cond_128).T,
        "W0": L0_cond_W0, "b0": np.asarray(L0_cond_b0).reshape(P, 1),
        "W1": L0_cond_W1, "b1": np.asarray(L0_cond_b1).reshape(P, 1),
        "W2": L0_cond_W2, "b2": np.asarray(L0_cond_b2).reshape(1, NE),
        "cw": np.asarray(L0_cond_weight).reshape(NE, T * T),
        "biask": L0_cond_bias_k,
        "cwT": np.asarray(L0_cond2_c_weight).T,
        "fside": np.tile(np.asarray(fside_S_0), BPT).reshape(P, 1),
        "wq": chunked(np.asarray(L0_attn_wq).T[:, pair]),
        "wk": chunked(np.asarray(L0_attn_wk).T[:, pair]),
        "wv": chunked(np.asarray(L0_attn_wv).T[:, v_cols]),
        "wo": chunked(np.asarray(L0_attn_wo).T[o_rows]),
        "wb": chunked(np.asarray(L0_ffn_W_base).T),
        "wa": chunked(np.asarray(L0_ffn_A).reshape(NA, C).T),
        "wg": chunked(np.asarray(L0_ffn_W_gate).T),
        "wbt": np.asarray(L0_ffn_B).transpose(0, 2, 1).reshape(NA, C),
        "bbase": np.asarray(L0_ffn_b_base).reshape(1, C),
        "wconv": conv.reshape(SH * T, TAPS // SH, T),
        "const": constants(),
    }
    arrays = {n: np.ascontiguousarray(a) for n, a in arrays.items()}
    nc = bacc.Bacc("TRN2", target_bir_lowering=False, num_devices=1)
    launch(nc, {n: a.shape for n, a in arrays.items()}, (B * T, C))
    r = run_bass_kernel_spmd(nc, [{"in_" + n: a for n, a in arrays.items()}], core_ids=[0])
    return r.results[0]["out_0"].reshape(B, T, C)
```

```python
import numpy as np
import concourse.bass as bass
from concourse import mybir
from contextlib import ExitStack

F32 = mybir.dt.float32
F32R = mybir.dt.float32r
U32 = mybir.dt.uint32
ALU = mybir.AluOpType
ACT = mybir.ActivationFunctionType
AX = mybir.AxisListType

P = 128
B, T, C = 128, 32, 512
H, HD = 32, 16
BPT = P // T
NT = B // BPT
TPM = 4
NM = NT // TPM
CK = C // P
MCOL = TPM * P
NE, RANK = 8, 16
NA = NE * RANK
NG = NA + NE
TAPS, PAD = 9, 4
SH = 3
XW = C + 2 * PAD
BANK = 512

C_ID, C_ROT, C_KM, C_IO, C_MASK = 0, 128, 134, 138, 146
NC = C_MASK + T


def build(nc, io):
    ctx = ExitStack()
    with ctx:
        def sb(name, shape, dt=F32):
            return ctx.enter_context(nc.sbuf_tensor(name, shape, dt))

        def sem(name):
            return ctx.enter_context(nc.semaphore(name))

        names = ["wq", "wk", "wv", "wo", "wb"]
        w_hi = {n: sb(n + "_hi", [P, CK, C], F32R) for n in names}
        w_lo = {n: sb(n + "_lo", [P, CK, C], F32R) for n in names}
        const = sb("const", [P, NC])
        wag = sb("wag", [P, CK, NG])
        wbt = sb("wbt", [P, 1, C])
        w_hi["wbt"] = sb("wbt_hi", [P, 1, C], F32R)
        w_lo["wbt"] = sb("wbt_lo", [P, 1, C], F32R)
        wconv = sb("wconv", [SH * T, TAPS // SH, T])
        bbase = sb("bbase", [P, C])
        mixT = sb("mixT", [P, NT, P])
        cbias = sb("cbias", [P, NT])
        xst = sb("xst", [P, CK, C])
        aggb = sb("aggb", [P, T])
        xin = sb("xin", [P, TPM, C])
        x1 = sb("x1", [P, C])
        x1b = sb("x1b", [P, 2, C])
        x3 = sb("x3", [SH * T, BPT, XW])
        aggbc = sb("aggbc", [P, MCOL])
        yf = sb("yf", [P, CK, P])
        yhi = sb("yhi", [P, CK, P], F32R)
        ylo = sb("ylo", [P, CK, P], F32R)
        qr = sb("qr", [P, C])
        kr = sb("kr", [P, C])
        qT = sb("qT", [P, CK, P])
        kT = sb("kT", [P, CK, P])
        kbd = sb("kbd", [P, CK, 4, P])
        vsb = sb("vsb", [P, 4, P])
        vbd = sb("vbd", [P, BPT, 4, P])
        es = sb("es", [P, H * T])
        pT = sb("pT", [P, H // 4, P])
        onat = sb("onat", [P, C])
        ohi = sb("ohi", [P, CK, P], F32R)
        olo = sb("olo", [P, CK, P], F32R)
        zsb = sb("zsb", [P, C])
        zTf = sb("zTf", [P, CK, P])
        zhi = sb("zhi", [P, CK, P], F32R)
        zlo = sb("zlo", [P, CK, P], F32R)
        zbias = sb("zbias", [P, 1])
        ost = sb("ost", [P, C])
        hw = sb("hw", [P, NA])
        hwT_hi = sb("hwT_hi", [P, 1, NA], F32R)
        hwT_lo = sb("hwT_lo", [P, 1, NA], F32R)
        rmx = sb("rmx", [P, H])
        rsum = sb("rsum", [P, H])
        rinv = sb("rinv", [P, H])
        r8 = sb("r8", [P, 72])
        ri = sb("ri", [P, 8], U32)

        ps = ctx.enter_context(nc.psum_tensor("ps", [P, 8 * BANK], F32))

        def bank(n, width=1):
            return ps[:, n * BANK:(n + width) * BANK]

        condT = kr[:, 0:B]
        W0, W1 = es[:, 0:128], es[:, 128:256]
        h1, h2 = es[:, 256:384], es[:, 384:512]
        W2 = es[:, 512:520]
        small = es[:, 520:600]
        cwsb = pT[:, :, :].rearrange("p a b -> p (a b)")[0:8, 0:T * T]
        attT = qr[0:8, 0:B]
        biask = qr[0:8, 128:160]
        cwT = kr[:, 128:128 + T]
        fside = kr[:, 160:161]
        stage = [xst[:, :, :]] + [t[:, :, :, :].rearrange("p a b c -> p a (b c)") for t in (vbd, kbd)]
        staged = {"wq": stage[0], "wk": stage[1], "wv": stage[2], "wo": stage[0], "wb": stage[0],
                  "wbt": wbt[:, :, :]}

        ident = const[:, C_ID:C_ID + P]
        rot = const[:, C_ROT:C_ROT + 6]
        kmask = const[:, C_KM:C_KM + 4]
        iota8 = const[:, C_IO:C_IO + 8]
        mask = const[:, C_MASK:C_MASK + T]

        ld_first, ld_second, ld_third = sem("ld_first"), sem("ld_second"), sem("ld_third")
        ld_cond, ld_const, ld_misc = sem("ld_cond"), sem("ld_const"), sem("ld_misc")
        ld_w = {n: sem("ld_" + n) for n in (*names, "wbt")}
        ld_x = [sem(f"ld_x{j}") for j in range(TPM)]
        whi_done = {n: sem(f"whi_{n}") for n in ld_w}
        wlo_done = {n: sem(f"wlo_{n}") for n in ld_w}
        table_in = sem("table_in")
        mix_ps, mix_a, mix_v = sem("mix_ps"), sem("mix_a"), sem("mix_v")
        zeroed, su_pe, su_act, su_dve = sem("zeroed"), sem("su_pe"), sem("su_act"), sem("su_dve")
        bias_out, bc_sb = sem("bias_out"), sem("bc_sb")
        cond_ps, y_f, y_hi, y_lo = sem("cond_ps"), sem("y_f"), sem("y_hi"), sem("y_lo")
        q_ps, k_ps, v_ps = sem("q_ps"), sem("k_ps"), sem("v_ps")
        q_cos, k_cos, v_sb, v_out, v_bd = (
            sem("q_cos"), sem("k_cos"), sem("v_sb"), sem("v_out"), sem("v_bd"))
        q_rot, k_rot = sem("q_rot"), sem("k_rot")
        tq_ps, tk_ps, qT_sb, kT_sb = sem("tq_ps"), sem("tk_ps"), sem("qT_sb"), sem("kT_sb")
        kbd_v, kbd_g = sem("kbd_v"), sem("kbd_g")
        s_mask = sem("s_mask")
        s_ps, s_max, s_sub, s_exp, s_sum, s_inv, p_norm = (
            sem("s_ps"), sem("s_max"), sem("s_sub"), sem("s_exp"), sem("s_sum"), sem("s_inv"), sem("p_norm"))
        pt_ps, pT_a, pT_v, pv_ps, o_sb = sem("pt_ps"), sem("pT_a"), sem("pT_v"), sem("pv_ps"), sem("o_sb")
        to_ps, o_hi, o_lo, wo_ps = sem("to_ps"), sem("o_hi"), sem("o_lo"), sem("wo_ps")
        x1_sb, x1b_sb, x1_out, x3_sb = sem("x1_sb"), sem("x1b_sb"), sem("x1_out"), sem("x3_sb")
        conv_ps, zb_sb, z_sb = sem("conv_ps"), sem("zb_sb"), sem("z_sb")
        tz_ps, z_f, z_hi, z_lo = sem("tz_ps"), sem("z_f"), sem("z_hi"), sem("z_lo")
        ag_ps, r_top, r_sub, r_exp, r_step, hw_sb = (
            sem("ag_ps"), sem("r_top"), sem("r_sub"), sem("r_exp"), sem("r_step"), sem("hw_sb"))
        ht_ps, hwT_sb, hwT_l, f_ps, f_out, stored = (
            sem("ht_ps"), sem("hwT_sb"), sem("hwT_l"), sem("f_ps"), sem("f_out"), sem("stored"))

        def need(eng, s, value):
            if isinstance(value, int) and value <= 0:
                return
            eng.wait_ge(s, value)

        def at(t, n=P):
            return slice(t * n, t * n + n) if isinstance(t, int) else bass.ds(t * n, n)

        def rows(eng, t):
            return at(t) if isinstance(t, int) else bass.ds(eng.snap(t * P), P)

        def run_slots(eng, slot):
            def four(m, first=False, last=False):
                for j in range(TPM):
                    slot(TPM * m + j, m, j, cur=True, prev=not (first and j == 0),
                         nxt=not (last and j == TPM - 1), ffn=not (first and j < 2),
                         end=not (first and j < 3))
            four(0, first=True)
            with eng.Fori(1, NM - 1) as m:
                four(m)
            four(NM - 1, last=True)
            slot(NT, NM, 0, cur=False, prev=True, nxt=False, ffn=True, end=True)
            slot(NT + 1, NM, 1, cur=False, prev=False, nxt=False, ffn=True, end=True)
            slot(NT + 2, NM, 2, cur=False, prev=False, nxt=False, ffn=False, end=True)

        def is_slot(t, n):
            return isinstance(t, int) and t == n

        def keep_mixing(eng, copy, half, batches, done):
            eng.wait_ge(mix_ps, half + 1)
            eng.wait_ge(zeroed, 1)
            for r in batches:
                own = slice(32 * r, 32 * r + 32)
                ins = copy(mixT[own, :, 32 * r + 16 * half:32 * r + 16 * half + 16],
                           bank(4 + half)[own, :].rearrange("i (o s) -> i s o", s=NT))
            ins.then_inc(done, 1)

        def split_low(eng, n):
            eng.wait_ge(whi_done[n], 1)
            eng.tensor_tensor(w_lo[n][:, :, :], staged[n], w_hi[n][:, :, :].bitcast(F32),
                              ALU.subtract).then_inc(wlo_done[n], 1)

        block = ctx.enter_context(nc.Block())

        @block.sync
        def _(sp):
            for dst, name in ((condT, "condT"), (W0, "W0"), (small[:, 0:1], "b0")):
                sp.dma_start(dst, io[name]).then_inc(ld_first, 16)
            for dst, name in ((W1, "W1"), (small[:, 1:2], "b1")):
                sp.dma_start(dst, io[name]).then_inc(ld_second, 16)
            sp.dma_start(W2, io["W2"]).then_inc(ld_third, 16)
            sp.dma_start(small[:, 8:16], io["b2"].to_broadcast([P, NE])).then_inc(ld_third, 16)
            for dst, name in ((biask, "biask"), (cwT, "cwT"), (fside, "fside")):
                sp.dma_start(dst, io[name]).then_inc(ld_cond, 16)
            sp.dma_start(cwsb, io["cw"]).then_inc(ld_cond, 16)
            sp.dma_start(xin[:, 0, :], io["x"][0:P, :]).then_inc(ld_x[0], 16)
            for n in ("wq", "wk", "wv"):
                sp.dma_start(staged[n], io[n]).then_inc(ld_w[n], 16)
            for j in range(1, TPM):
                sp.dma_start(xin[:, j, :], io["x"][at(j), :]).then_inc(ld_x[j], 16)
            sp.wait_ge(su_dve, 8)
            sp.dma_start(io["mixbias"].rearrange("m (b t) -> (m b) t", t=T), aggb[:, :]).then_inc(bias_out, 16)
            sp.wait_ge(bias_out, 16)
            sp.dma_start(aggbc[:, :], io["mixbias"][0:1, :].to_broadcast([P, MCOL])).then_inc(bc_sb, 16)
            sp.dma_start(wconv[:, :, :], io["wconv"]).then_inc(ld_misc, 16)
            sp.dma_start(wag[:, :, 0:NA], io["wa"]).then_inc(ld_misc, 16)
            sp.dma_start(wag[:, :, NA:NG], io["wg"]).then_inc(ld_misc, 16)
            sp.dma_start(wbt[:, 0, :], io["wbt"]).then_inc(ld_w["wbt"], 16)
            sp.dma_start(bbase[:, :], io["bbase"].to_broadcast([P, C])).then_inc(ld_misc, 16)

            def load_late(n, before):
                sp.wait_ge(whi_done[before], 1)
                sp.wait_ge(wlo_done[before], 1)
                sp.dma_start(staged[n], io[n]).then_inc(ld_w[n], 16)

            load_late("wo", "wq")

            values = io["values"].rearrange("(b t) h c -> t b h c", t=T)
            tokens = io["x1"].rearrange("(b t) c -> t b c", t=T)

            def slot(t, m, j, cur, prev, nxt, ffn, end):
                more = prev and not (isinstance(t, int) and t + TPM - 1 >= NT)
                x_rows = rows(sp, t + TPM - 1) if more else None
                out_rows = rows(sp, t - 3) if end else None
                if nxt and j == TPM - 1:
                    of_next = (slice(m + 1, m + 2) if isinstance(m, int) else bass.ds(sp.snap(m + 1), 1))
                    sp.wait_ge(y_f, t + 1)
                    sp.dma_start(aggbc[:, :], io["mixbias"][of_next, :].to_broadcast([P, MCOL])).then_inc(bc_sb, 16)
                if end:
                    sp.wait_ge(f_out, t - 2)
                    sp.dma_start(io["out"][out_rows, :], ost[:, :]).then_inc(stored, 16)
                if cur:
                    sp.wait_ge(v_sb, t + 1)
                    sp.dma_start(io["values"], vsb[:, :, :]).then_inc(v_out, 16)
                    sp.wait_ge(v_out, 16 * (t + 1))
                    need(sp, pv_ps, t)
                    if is_slot(t, 0):
                        sp.wait_ge(zeroed, 4)
                    for h in range(4):
                        sp.dma_start(vbd[32 * h:32 * h + 32, :, h, :], values[:, :, h, :]).then_inc(v_bd, 16)
                if is_slot(t, 1):
                    load_late("wb", "wo")
                if prev:
                    sp.wait_ge(x1_sb, t)
                    sp.dma_start(io["x1"], x1[:, :]).then_inc(x1_out, 16)
                    sp.wait_ge(x1_out, 16 * t)
                    if not cur:
                        sp.wait_ge(conv_ps, t - 1)
                    for shift in range(SH):
                        sp.dma_start(x3[32 * shift:32 * shift + 32, :, PAD - shift:PAD - shift + C],
                                     tokens).then_inc(x3_sb, 16)
                    if more:
                        jn = (j - 1) % TPM
                        sp.dma_start(xin[:, jn, :], io["x"][x_rows, :]).then_inc(ld_x[jn], 16)

            run_slots(sp, slot)
            sp.wait_ge(stored, 16 * NT)

        @block.tensor
        def _(pe):
            def split_mm(out, hi, lo, name, low, tile, first=True, last=True):
                chunks = hi.shape[1]
                for a, (x, w) in enumerate(((hi, w_hi[name]), (hi, w_lo[name]), (lo, w_hi[name]))):
                    if a == 2:
                        pe.wait_ge(low, tile + 1)
                    for c in range(chunks):
                        mm = pe.matmul(out, x[:, c, :], w[:, c, :], start=(first and a == 0 and c == 0),
                                       stop=(last and a == 2 and c == chunks - 1), skip_group_check=True)
                return mm

            def turn(n, src, done):
                for c in range(CK):
                    mm = pe.transpose(bank(n)[:, c * P:(c + 1) * P], src[:, c * P:(c + 1) * P], ident)
                mm.then_inc(done, 1)

            def mix(t, m, j):
                pe.wait_ge(ld_x[j], 16 * (m + 1))
                mixing = mixT[:, t, :] if isinstance(t, int) else \
                    mixT[:, bass.ds(t, 1), :].rearrange("p o c -> p (o c)")
                for c in range(CK):
                    mm = pe.matmul(bank(7)[:, c * P:(c + 1) * P], xin[:, j, c * P:(c + 1) * P], mixing,
                                   start=True, stop=True, skip_group_check=True)
                mm.then_inc(cond_ps, 1)

            def weights(name):
                pe.wait_ge(whi_done[name], 1)
                pe.wait_ge(wlo_done[name], 1)

            def convolve(t, cur):
                if is_slot(t, 2):
                    pe.wait_ge(ld_misc, 16 * 4)
                pe.wait_ge(x3_sb, 16 * SH * (t - 1))
                if cur:
                    pe.wait_ge(q_rot, t + 1)
                else:
                    pe.wait_ge(o_lo, min(t, NT))
                for g in range(TAPS // SH):
                    for b in range(BPT):
                        mm = pe.matmul(bank(6)[32 * b:32 * b + 32, :], wconv[:, g, :],
                                       x3[:, b, SH * g:SH * g + C], start=(g == 0),
                                       stop=(g == TAPS // SH - 1), skip_group_check=True)
                mm.then_inc(conv_ps, 1)

            def turn_convolved(t, cur):
                pe.wait_ge(z_sb, t - 1)
                if cur:
                    pe.wait_ge(v_sb, t + 1)
                turn(5, zsb, tz_ps)

            def gate(t):
                pe.wait_ge(z_f, t - 1)
                for c in range(CK):
                    mm = pe.matmul(bank(5)[:, 0:NG], zTf[:, c, :], wag[:, c, :],
                                   start=(c == 0), stop=(c == CK - 1), skip_group_check=True)
                mm.then_inc(ag_ps, 1)

            def slot(t, m, j, cur, prev, nxt, ffn, end):
                if cur:
                    if is_slot(t, 0):
                        weights("wq")
                    pe.wait_ge(y_hi, t + 1)
                    need(pe, o_lo, t - 1)
                    split_mm(bank(6), yhi, ylo, "wq", y_lo, t).then_inc(q_ps, 1)
                if end:
                    pe.wait_ge(hw_sb, t - 2)
                    pe.transpose(bank(5)[:, 256:256 + NA], hw[:, :], ident).then_inc(ht_ps, 1)
                if cur:
                    if is_slot(t, 0):
                        weights("wk")
                    need(pe, o_sb, t - 1)
                    split_mm(bank(4), yhi, ylo, "wk", y_lo, t).then_inc(k_ps, 1)
                if end:
                    if is_slot(t, 3):
                        weights("wbt")
                    pe.wait_ge(hwT_sb, t - 2)
                    split_mm(bank(2), hwT_hi, hwT_lo, "wbt", hwT_l, t - 3, first=False).then_inc(f_ps, 1)
                if cur:
                    if is_slot(t, 0):
                        weights("wv")
                    split_mm(bank(5), yhi, ylo, "wv", y_lo, t).then_inc(v_ps, 1)
                if cur:
                    pe.wait_ge(q_rot, t + 1)
                    need(pe, f_out, t - 2)
                    turn(2, qr, tq_ps)
                    pe.wait_ge(k_rot, t + 1)
                    turn(3, kr, tk_ps)
                if prev:
                    pe.wait_ge(p_norm, t)
                    for g in range(H // 4):
                        mm = pe.transpose(bank(0, 2)[:, g * P:(g + 1) * P], es[:, g * P:(g + 1) * P], ident)
                    mm.then_inc(pt_ps, 1)
                if ffn and cur:
                    convolve(t, cur)
                if prev:
                    pe.wait_ge(pT_a, t)
                    pe.wait_ge(pT_v, t)
                    pe.wait_ge(v_bd, 16 * 4 * t)
                    if cur:
                        pe.wait_ge(k_rot, t + 1)
                    for g in range(H // 4):
                        for b in range(BPT):
                            mm = pe.matmul(bank(4)[32 * b:32 * b + 32, g * 64:(g + 1) * 64],
                                           pT[:, g, 32 * b:32 * b + 32], vbd[:, b, :, g * HD:(g + 1) * HD],
                                           start=True, stop=True, skip_group_check=True)
                    mm.then_inc(pv_ps, 1)
                if ffn and cur:
                    turn_convolved(t, cur)
                if nxt:
                    need(pe, x1_sb, t - 1)
                    mix(t + 1, m + (j + 1) // TPM, (j + 1) % TPM)
                if prev:
                    pe.wait_ge(o_sb, t)
                    need(pe, z_sb, t - 1 if cur else t - 2)
                    turn(6, onat, to_ps)
                if ffn and cur:
                    gate(t)
                if cur:
                    pe.wait_ge(su_pe, 6)
                    pe.wait_ge(qT_sb, t + 1)
                    pe.wait_ge(kbd_v, t + 1)
                    pe.wait_ge(kbd_g, t + 1)
                    if prev:
                        pe.wait_ge(pT_a, t)
                        pe.wait_ge(pT_v, t)
                    for c in range(CK):
                        for g in range(2):
                            for b in range(BPT):
                                mm = pe.matmul(
                                    bank(g)[32 * b:32 * b + 32, c * P:(c + 1) * P],
                                    qT[64 * g:64 * g + 64, c, 32 * b:32 * b + 32],
                                    kbd[64 * g:64 * g + 64, c, :, 32 * b:32 * b + 32],
                                    start=True, stop=True, skip_group_check=True)
                    mm.then_inc(s_ps, 1)
                if prev:
                    if is_slot(t, 1):
                        weights("wo")
                    pe.wait_ge(o_hi, t)
                    if nxt:
                        pe.wait_ge(y_f, t + 2)
                    split_mm(bank(7), ohi, olo, "wo", o_lo, t - 1).then_inc(wo_ps, 1)
                if ffn and not cur:
                    convolve(t, cur)
                    turn_convolved(t, cur)
                    gate(t)
                if ffn:
                    if is_slot(t, 2):
                        weights("wb")
                    pe.wait_ge(z_hi, t - 1)
                    if cur:
                        pe.wait_ge(qT_sb, t + 1)
                    else:
                        pe.wait_ge(f_out, t - 2)
                    split_mm(bank(2), zhi, zlo, "wb", z_lo, t - 2, last=False)

            pe.wait_ge(ld_first, 16 * 3)
            pe.matmul(bank(0)[:, 0:P], W0, condT, start=True, stop=True).then_inc(su_pe, 1)
            pe.wait_ge(ld_second, 16 * 2)
            pe.wait_ge(su_act, 1)
            pe.matmul(bank(1)[:, 0:P], W1, h1, start=True, stop=True).then_inc(su_pe, 1)
            pe.wait_ge(su_act, 2)
            pe.wait_ge(ld_third, 16 * 2)
            pe.matmul(bank(2)[:, 0:NE], h2, W2, start=True, stop=True).then_inc(su_pe, 1)
            pe.wait_ge(ld_cond, 16 * 4)
            condv = condT.rearrange("d (s r) -> d r s", r=BPT)
            for r in range(BPT):
                mm = pe.matmul(bank(6)[32 * r:32 * r + 32, 0:NT], cwT, condv[:, r, :],
                               start=True, stop=True, skip_group_check=True)
            mm.then_inc(su_pe, 1)
            pe.wait_ge(su_dve, 6)
            pe.wait_ge(ld_const, 16)
            pe.transpose(bank(3)[0:NE, 0:P], small[:, 24:32], ident).then_inc(su_pe, 1)
            pe.wait_ge(su_dve, 7)
            pe.matmul(bank(2)[:, 16:16 + T], attT, biask, start=True, stop=True).then_inc(su_pe, 1)
            cwv = cwsb.rearrange("k (o i) -> k o i", i=T)
            attv = attT.rearrange("k (s r) -> k r s", r=BPT)
            for half in range(2):
                for o in range(T // 2 * half, T // 2 * (half + 1)):
                    for r in range(BPT):
                        mm = pe.matmul(bank(4, 2)[32 * r:32 * r + 32, o * NT:(o + 1) * NT], cwv[:, o, :],
                                       attv[:, r, :], start=True, stop=True, skip_group_check=True)
                mm.then_inc(mix_ps, 1)
            pe.wait_ge(mix_a, 2)
            pe.wait_ge(mix_v, 2)
            mix(0, 0, 0)
            run_slots(pe, slot)

        @block.scalar
        def _(act):
            def y_high(t):
                act.wait_ge(y_f, t + 1)
                need(act, v_ps, t)
                act.copy(yhi[:, :, :], yf[:, :, :]).then_inc(y_hi, 1)

            def four(n):
                return bank(n).rearrange("p (c r) -> p c r", c=CK)

            def high(n):
                act.wait_ge(ld_w[n], 16)
                act.copy(w_hi[n][:, :, :], staged[n]).then_inc(whi_done[n], 1)

            def add_bias(t):
                act.wait_ge(conv_ps, t - 1)
                act.wait_ge(zb_sb, t - 1)
                need(act, tz_ps, t - 2)
                act.activation(zsb[:, :], bank(6), ACT.Identity, bias=zbias[:, 0:1]).then_inc(z_sb, 1)

            def keep_turned(t):
                act.wait_ge(tz_ps, t - 1)
                need(act, ag_ps, t - 2)
                need(act, z_lo, t - 2)
                act.copy(zTf[:, :, :], four(5)).then_inc(z_f, 1)

            def slot(t, m, j, cur, prev, nxt, ffn, end):
                if cur:
                    act.wait_ge(q_ps, t + 1)
                    need(act, tq_ps, t)
                    act.activation(qr[:, :], bank(6), ACT.Copy, scale=rot[:, 0:1]).then_inc(q_cos, 1)
                if end:
                    act.wait_ge(ht_ps, t - 2)
                    need(act, f_ps, t - 3)
                    act.copy(hwT_hi[:, 0, :], bank(5)[:, 256:256 + NA]).then_inc(hwT_sb, 1)
                if cur:
                    act.wait_ge(k_ps, t + 1)
                    need(act, tk_ps, t)
                    act.activation(kr[:, :], bank(4), ACT.Copy, scale=rot[:, 3:4]).then_inc(k_cos, 1)
                    if is_slot(t, 1):
                        high("wo")
                    act.wait_ge(v_ps, t + 1)
                    need(act, v_bd, 16 * 4 * t)
                    act.copy(vsb[:, :, :], four(5)).then_inc(v_sb, 1)
                    act.wait_ge(tq_ps, t + 1)
                    need(act, s_ps, t)
                    act.copy(qT[:, :, :], four(2)).then_inc(qT_sb, 1)
                    act.wait_ge(tk_ps, t + 1)
                    need(act, kbd_v, t)
                    need(act, kbd_g, t)
                    act.copy(kT[:, :, :], four(3)).then_inc(kT_sb, 1)
                if prev:
                    act.wait_ge(pt_ps, t)
                    need(act, pv_ps, t - 1)
                    act.copy(pT[:, 0:4, :], four(0)).then_inc(pT_a, 1)
                if is_slot(t, 2):
                    high("wb")
                    high("wbt")
                if ffn and cur:
                    add_bias(t)
                if prev:
                    act.wait_ge(pv_ps, t)
                    need(act, to_ps, t - 1)
                    act.copy(onat[:, :], bank(4)).then_inc(o_sb, 1)
                if ffn and cur:
                    keep_turned(t)
                if nxt:
                    y_high(t + 1)
                if prev:
                    act.wait_ge(to_ps, t)
                    need(act, wo_ps, t - 1)
                    act.copy(ohi[:, :, :], four(6)).then_inc(o_hi, 1)
                if ffn and not cur:
                    add_bias(t)
                    keep_turned(t)
                if ffn:
                    act.wait_ge(r_sub, t - 1)
                    act.activation(r8[:, 16:24], r8[:, 8:16], ACT.Exp).then_inc(r_exp, 1)
                if cur:
                    act.wait_ge(s_sub, t + 1)
                    act.activation(es[:, :], es[:, :], ACT.Exp).then_inc(s_exp, 1)

            act.dma_start(const[:, :], io["const"]).then_inc(ld_const, 16)
            act.wait_ge(table_in, 1)
            act.activation(small[:, 57:58], small[:, 56:57], ACT.Gelu)
            act.wait_ge(ld_first, 16 * 3)
            act.wait_ge(su_pe, 1)
            act.activation(h1, bank(0)[:, 0:P], ACT.Gelu, bias=small[:, 0:1]).then_inc(su_act, 1)
            act.wait_ge(ld_second, 16 * 2)
            act.wait_ge(su_pe, 2)
            act.activation(h2, bank(1)[:, 0:P], ACT.Gelu, bias=small[:, 1:2]).then_inc(su_act, 1)
            act.wait_ge(su_dve, 3)
            act.activation(small[:, 32:40], small[:, 16:24], ACT.Exp).then_inc(su_act, 1)
            high("wq")
            high("wk")
            for half in range(2):
                keep_mixing(act, act.copy, half, (0, 1), mix_a)
            y_high(0)
            high("wv")
            run_slots(act, slot)

        @block.vector
        def _(dve):
            def four(n):
                return bank(n).rearrange("p (c r) -> p c r", c=CK)

            def rotate(dst, src, k, done):
                d = dst[:, :].rearrange("p (h two e) -> p h two e", two=2, e=HD // 2)
                s = src.rearrange("p (h two e) -> p h two e", two=2, e=HD // 2)
                dve.scalar_tensor_tensor(out=d[:, :, 0, :], in0=s[:, :, 1, :], scalar=rot[:, k + 2:k + 3],
                                         in1=d[:, :, 0, :], op0=ALU.mult, op1=ALU.add)
                dve.scalar_tensor_tensor(out=d[:, :, 1, :], in0=s[:, :, 0, :], scalar=rot[:, k + 1:k + 2],
                                         in1=d[:, :, 1, :], op0=ALU.mult, op1=ALU.add).then_inc(done, 1)

            def y_full(t, m, j):
                dve.wait_ge(cond_ps, t + 1)
                need(dve, y_hi, t)
                need(dve, y_lo, t)
                if j == 0:
                    dve.wait_ge(bc_sb, 16 * (m + 1))
                dve.tensor_tensor(yf[:, :, :], four(7),
                                  aggbc[:, None, j * P:(j + 1) * P].to_broadcast([P, CK, P]),
                                  ALU.add).then_inc(y_f, 1)

            def z_high(t):
                dve.wait_ge(z_f, t - 1)
                need(dve, f_ps, t - 2)
                dve.tensor_copy(zhi[:, :, :], zTf[:, :, :]).then_inc(z_hi, 1)

            def route(t):
                f = t - 2
                dve.wait_ge(ag_ps, f + 1)
                dve.tensor_reduce(r8[:, 0:1], bank(5)[:, NA:NG], AX.X, ALU.max).then_inc(r_top, 1)
                dve.wait_ge(r_top, 2 * f + 1)
                need(dve, r_exp, f)
                dve.tensor_scalar(r8[:, 8:16], bank(5)[:, NA:NG], r8[:, 0:1], None,
                                  ALU.subtract).then_inc(r_sub, 1)
                dve.wait_ge(su_dve, 9)
                dve.wait_ge(r_exp, f + 1)
                dve.max(r8[:, 24:32], r8[:, 16:24]).then_inc(r_top, 1)
                dve.wait_ge(r_top, 2 * f + 2)
                dve.tensor_tensor(r8[:, 64:65], r8[:, 24:25], r8[:, 25:26], ALU.add).then_inc(r_step, 1)
                dve.max_index(ri[:, :], r8[:, 24:32], r8[:, 16:24]).then_inc(r_step, 1)
                dve.wait_ge(r_step, 6 * f + 2)
                dve.tensor_copy(r8[:, 32:40], ri[:, :]).then_inc(r_step, 1)
                dve.reciprocal(r8[:, 65:66], r8[:, 64:65])
                dve.wait_ge(r_step, 6 * f + 3)
                dve.tensor_scalar(r8[:, 40:48], iota8, r8[:, 32:33], r8[:, 24:25], ALU.is_equal,
                                  ALU.mult).then_inc(r_step, 1)
                dve.tensor_scalar(r8[:, 48:56], iota8, r8[:, 33:34], r8[:, 25:26], ALU.is_equal,
                                  ALU.mult).then_inc(r_step, 1)
                dve.wait_ge(r_step, 6 * f + 5)
                dve.tensor_tensor(r8[:, 56:64], r8[:, 40:48], r8[:, 48:56], ALU.add).then_inc(r_step, 1)
                dve.wait_ge(r_step, 6 * f + 6)
                need(dve, ht_ps, f)
                dve.scalar_tensor_tensor(out=hw[:, :].rearrange("p (e r) -> p e r", e=NE),
                                         in0=bank(5)[:, 0:NA].rearrange("p (e r) -> p e r", e=NE),
                                         scalar=r8[:, 65:66],
                                         in1=r8[:, 56:64, None].to_broadcast([P, NE, RANK]),
                                         op0=ALU.mult, op1=ALU.mult).then_inc(hw_sb, 1)

            def slot(t, m, j, cur, prev, nxt, ffn, end):
                if cur:
                    dve.wait_ge(q_cos, t + 1)
                    rotate(qr, bank(6), 0, q_rot)
                if end:
                    dve.wait_ge(hwT_sb, t - 2)
                    need(dve, f_ps, t - 3)
                    dve.tensor_tensor(hwT_lo[:, 0, :], bank(5)[:, 256:256 + NA], hwT_hi[:, 0, :].bitcast(F32),
                                      ALU.subtract).then_inc(hwT_l, 1)
                if cur:
                    dve.wait_ge(k_cos, t + 1)
                    rotate(kr, bank(4), 3, k_rot)
                if end:
                    dve.wait_ge(f_ps, t - 2)
                    dve.wait_ge(x1b_sb, t - 2)
                    need(dve, stored, 16 * (t - 3))
                    dve.tensor_tensor(ost[:, :], bank(2), x1b[:, (j - 3) % 2, :], ALU.add).then_inc(f_out, 1)
                if prev:
                    dve.wait_ge(pt_ps, t)
                    need(dve, pv_ps, t - 1)
                    dve.tensor_copy(pT[:, 4:8, :], four(1)).then_inc(pT_v, 1)
                if cur:
                    dve.wait_ge(kT_sb, t + 1)
                    need(dve, s_ps, t)
                    if is_slot(t, 0):
                        dve.wait_ge(wlo_done["wv"], 1)
                    for h in range(3):
                        ins = dve.tensor_scalar(kbd[:, :, h, :], kT[:, :, :], kmask[:, h:h + 1], None, ALU.mult)
                    ins.then_inc(kbd_v, 1)
                if nxt:
                    y_full(t + 1, m + (j + 1) // TPM, (j + 1) % TPM)
                if ffn and cur:
                    z_high(t)
                if prev:
                    dve.wait_ge(o_hi, t)
                    need(dve, wo_ps, t - 1)
                    dve.tensor_tensor(olo[:, :, :], four(6), ohi[:, :, :].bitcast(F32),
                                      ALU.subtract).then_inc(o_lo, 1)
                if ffn and cur:
                    route(t)
                if cur:
                    s3 = bank(0, 2).rearrange("p (h k) -> p h k", k=T)
                    e3 = es[:, :].rearrange("p (h k) -> p h k", k=T)
                    dve.wait_ge(s_ps, t + 1)
                    need(dve, pt_ps, t)
                    dve.tensor_tensor(e3, s3, mask[:, None, :].to_broadcast([P, H, T]),
                                      ALU.add).then_inc(s_mask, 1)
                    dve.wait_ge(s_mask, t + 1)
                    dve.tensor_reduce(rmx[:, :], e3, AX.X, ALU.max).then_inc(s_max, 1)
                    dve.wait_ge(s_max, t + 1)
                    dve.tensor_tensor(e3, e3, rmx[:, :, None].to_broadcast([P, H, T]),
                                      ALU.subtract).then_inc(s_sub, 1)
                if prev:
                    dve.wait_ge(wo_ps, t)
                    need(dve, x3_sb, 16 * SH * (t - 1))
                    need(dve, x1b_sb, t - 1)
                    dve.tensor_tensor(x1[:, :], bank(7), xin[:, (j - 1) % TPM, :],
                                      ALU.add).then_inc(x1_sb, 1)
                if ffn and not cur:
                    z_high(t)
                    route(t)
                if cur:
                    dve.wait_ge(s_exp, t + 1)
                    dve.tensor_reduce(rsum[:, :], e3, AX.X, ALU.add).then_inc(s_sum, 1)
                    dve.wait_ge(s_sum, t + 1)
                    need(dve, p_norm, t)
                    dve.reciprocal(rinv[:, :], rsum[:, :]).then_inc(s_inv, 1)

            lg, mx, e8, att = small[:, 16:24], small[:, 40:48], small[:, 32:40], small[:, 24:32]
            dve.wait_ge(ld_third, 16 * 2)
            dve.wait_ge(su_pe, 3)
            dve.tensor_tensor(lg, bank(2)[:, 0:NE], small[:, 8:16], ALU.add).then_inc(su_dve, 1)
            dve.wait_ge(su_dve, 1)
            dve.max(mx, lg).then_inc(su_dve, 1)
            dve.wait_ge(su_dve, 2)
            dve.tensor_scalar(lg, lg, mx[:, 0:1], None, ALU.subtract).then_inc(su_dve, 1)
            dve.wait_ge(su_act, 3)
            dve.tensor_reduce(small[:, 48:49], e8, AX.X, ALU.add).then_inc(su_dve, 1)
            dve.wait_ge(su_dve, 4)
            dve.reciprocal(small[:, 49:50], small[:, 48:49]).then_inc(su_dve, 1)
            dve.wait_ge(su_dve, 5)
            dve.tensor_scalar(att, e8, small[:, 49:50], None, ALU.mult).then_inc(su_dve, 1)
            dve.wait_ge(su_pe, 5)
            dve.tensor_copy(attT, bank(3)[0:NE, 0:P]).then_inc(su_dve, 1)
            dve.wait_ge(su_pe, 6)
            dve.tensor_copy(aggb[:, :], bank(2)[:, 16:16 + T]).then_inc(su_dve, 1)
            dve.wait_ge(su_pe, 4)
            dve.wait_ge(ld_cond, 16 * 4)
            dve.tensor_scalar(cbias[:, :], bank(6)[:, 0:NT], fside, None, ALU.add).then_inc(su_dve, 1)
            split_low(dve, "wq")
            keep_mixing(dve, dve.tensor_copy, 0, (2, 3), mix_v)
            split_low(dve, "wk")
            keep_mixing(dve, dve.tensor_copy, 1, (2, 3), mix_v)
            y_full(0, 0, 0)
            split_low(dve, "wv")
            run_slots(dve, slot)

        @block.gpsimd
        def _(pool):
            def y_low(t):
                pool.wait_ge(y_hi, t + 1)
                need(pool, v_ps, t)
                pool.tensor_tensor(ylo[:, :, :], yf[:, :, :], yhi[:, :, :].bitcast(F32),
                                   ALU.subtract).then_inc(y_lo, 1)

            def z_low(t):
                pool.wait_ge(z_hi, t - 1)
                need(pool, f_ps, t - 2)
                pool.tensor_tensor(zlo[:, :, :], zTf[:, :, :], zhi[:, :, :].bitcast(F32),
                                   ALU.subtract).then_inc(z_lo, 1)

            def slot(t, m, j, cur, prev, nxt, ffn, end):
                if ffn:
                    need(pool, z_sb, t - 2)
                    pool.tensor_copy(zbias[:, :], cbias[:, at(t - 2, 1)]).then_inc(zb_sb, 1)
                if cur:
                    pool.wait_ge(kT_sb, t + 1)
                    need(pool, s_ps, t)
                    if is_slot(t, 0):
                        pool.wait_ge(wlo_done["wv"], 1)
                    pool.tensor_tensor(kbd[:, :, 3, :], kT[:, :, :],
                                       kmask[:, 3:4, None].to_broadcast([P, CK, P]), ALU.mult).then_inc(kbd_g, 1)
                if is_slot(t, 1):
                    split_low(pool, "wo")
                if is_slot(t, 2):
                    split_low(pool, "wb")
                    split_low(pool, "wbt")
                if nxt:
                    y_low(t + 1)
                if ffn and cur:
                    z_low(t)
                if prev:
                    if is_slot(t, 1):
                        pool.wait_ge(ld_misc, 16 * 4)
                    pool.wait_ge(x1_sb, t)
                    need(pool, f_out, t - 2)
                    pool.tensor_tensor(x1b[:, (j - 1) % 2, :], x1[:, :], bbase[:, :],
                                       ALU.add).then_inc(x1b_sb, 1)
                if ffn and not cur:
                    z_low(t)
                if cur:
                    pool.wait_ge(s_inv, t + 1)
                    e3 = es[:, :].rearrange("p (h k) -> p h k", k=T)
                    pool.tensor_tensor(e3, e3, rinv[:, :, None].to_broadcast([P, H, T]),
                                       ALU.mult).then_inc(p_norm, 1)

            pool.memset(small[:, 56:57], 0.0).then_inc(table_in, 1)
            pool.memset(mixT[:, :, :], 0.0).then_inc(zeroed, 1)
            pool.memset(x3[:, :, :], 0.0).then_inc(zeroed, 1)
            y_low(0)
            pool.wait_ge(whi_done["wk"], 1)
            pool.wait_ge(wlo_done["wk"], 1)
            pool.memset(vbd[:, :, :, :], 0.0).then_inc(zeroed, 2)
            pool.wait_ge(su_dve, 9)
            run_slots(pool, slot)


def launch(nc, shapes, out_shape):
    io = {n: nc.dram_tensor("in_" + n, s, F32, kind="ExternalInput").ap() for n, s in shapes.items()}
    io["values"] = nc.dram_tensor("values_moved", (P, 4, P), F32, kind="Internal").ap()
    io["x1"] = nc.dram_tensor("x1_moved", (P, C), F32, kind="Internal").ap()
    io["mixbias"] = nc.dram_tensor("mixbias", (NM, MCOL), F32, kind="Internal").ap()
    io["out"] = nc.dram_tensor("out_0", out_shape, F32, kind="ExternalOutput").ap()
    build(nc, io)


def constants():
    c = np.zeros((P, NC), np.float32)
    p = np.arange(P)
    c[:, C_ID:C_ID + P] = np.eye(P)
    angle = (p % T).astype(np.float32)
    cos, sin, scale = np.cos(angle), np.sin(angle), np.float32(HD ** -0.5)
    for n, v in enumerate((cos * scale, sin * scale, -sin * scale, cos, sin, -sin)):
        c[:, C_ROT + n] = v
    for h in range(4):
        c[:, C_KM + h] = (p // HD) % 4 == h
    c[:, C_IO:C_IO + 8] = np.arange(8)
    c[:, C_MASK:C_MASK + T] = np.where(np.arange(T)[None, :] <= (p % T)[:, None], 0.0, -1e30)
    return c


def kernel(x, cond_128, fside_S_0, L0_cond_W0, L0_cond_b0, L0_cond_W1, L0_cond_b1, L0_cond_W2, L0_cond_b2,
           L0_cond_weight, L0_cond_bias_k, L0_attn_wq, L0_attn_wk, L0_attn_wv, L0_attn_wo, L0_cond2_weight,
           L0_cond2_c_weight, L0_ffn_W_base, L0_ffn_b_base, L0_ffn_W_gate, L0_ffn_A, L0_ffn_B):
    import concourse.bacc as bacc
    from concourse.bass_utils import run_bass_kernel_spmd

    def chunked(w):
        return w.reshape(CK, P, -1).transpose(1, 0, 2)

    pair = np.arange(C).reshape(H, HD // 2, 2).transpose(0, 2, 1).reshape(-1)
    heads = np.arange(H).reshape(CK, 2, 4).transpose(1, 0, 2)
    v_cols = (heads.transpose(2, 0, 1)[..., None] * HD + np.arange(HD)).reshape(-1)
    o_rows = (heads[..., None] * HD + np.arange(HD)).reshape(-1)

    wc = np.asarray(L0_cond2_weight).reshape(T, 8, TAPS // SH, SH)
    conv = np.zeros((SH, T, TAPS // SH, T), np.float32)
    for g in range(4):
        own = slice(8 * g, 8 * g + 8)
        conv[:, own, :, own] = wc[own].transpose(3, 1, 2, 0)

    arrays = {
        "x": np.asarray(x).reshape(B * T, C),
        "condT": np.asarray(cond_128).T,
        "W0": L0_cond_W0, "b0": np.asarray(L0_cond_b0).reshape(P, 1),
        "W1": L0_cond_W1, "b1": np.asarray(L0_cond_b1).reshape(P, 1),
        "W2": L0_cond_W2, "b2": np.asarray(L0_cond_b2).reshape(1, NE),
        "cw": np.asarray(L0_cond_weight).reshape(NE, T * T),
        "biask": L0_cond_bias_k,
        "cwT": np.asarray(L0_cond2_c_weight).T,
        "fside": np.tile(np.asarray(fside_S_0), BPT).reshape(P, 1),
        "wq": chunked(np.asarray(L0_attn_wq).T[:, pair]),
        "wk": chunked(np.asarray(L0_attn_wk).T[:, pair]),
        "wv": chunked(np.asarray(L0_attn_wv).T[:, v_cols]),
        "wo": chunked(np.asarray(L0_attn_wo).T[o_rows]),
        "wb": chunked(np.asarray(L0_ffn_W_base).T),
        "wa": chunked(np.asarray(L0_ffn_A).reshape(NA, C).T),
        "wg": chunked(np.asarray(L0_ffn_W_gate).T),
        "wbt": np.asarray(L0_ffn_B).transpose(0, 2, 1).reshape(NA, C),
        "bbase": np.asarray(L0_ffn_b_base).reshape(1, C),
        "wconv": conv.reshape(SH * T, TAPS // SH, T),
        "const": constants(),
    }
    arrays = {n: np.ascontiguousarray(a) for n, a in arrays.items()}
    nc = bacc.Bacc("TRN2", target_bir_lowering=False, num_devices=1)
    launch(nc, {n: a.shape for n, a in arrays.items()}, (B * T, C))
    r = run_bass_kernel_spmd(nc, [{"in_" + n: a for n, a in arrays.items()}], core_ids=[0])
    return r.results[0]["out_0"].reshape(B, T, C)
```
